# Optimizing a Trainium2 kernel written in Bass

```python
import numpy as np
import jax
import jax.numpy as jnp

def _softmax(x, axis=-1):
    return jax.nn.softmax(x, axis=axis)

def _gelu(x):
    return jax.nn.gelu(x, approximate=True)

def _silu(x):
    return jax.nn.silu(x)

def _sigmoid(x):
    return jax.nn.sigmoid(x)

def _layernorm(x, axis=-1, eps=1e-05):
    m = jnp.mean(x, axis=axis, keepdims=True)
    v = jnp.var(x, axis=axis, keepdims=True)
    return (x - m) / jnp.sqrt(v + eps)

def _scatter_add(tgt, idx, src, axis=0):
    return tgt.at[idx].add(src)

def _segment_sum(src, seg, n):
    return jax.ops.segment_sum(src, seg, n)
kernel_name = 'mk_macaron_d1_jaxref_r8_abf78f'

def setup_inputs(seed: int=0):
    np.random.seed(seed)
    _w = jnp.asarray

    def _L0_attn_setup():
        import jax, jax.numpy as jnp
        import numpy as np
        D_MODEL = 128
        N_HEADS = 16
        HEAD_DIM = D_MODEL // N_HEADS
        SCALE = HEAD_DIM ** (-0.5)
        MIN_VAL = jnp.finfo(jnp.float32).min

        def _split_heads(y):
            B, T, _ = y.shape
            return y.reshape(B, T, N_HEADS, HEAD_DIM).transpose(0, 2, 1, 3)
        key = jax.random.key(seed)
        ks = jax.random.split(key, 7)
        B, T = (1, 256)
        s = D_MODEL ** (-0.5)
        return {'x': jax.random.normal(ks[0], (B, T, D_MODEL), dtype=jnp.float32), 'Wq': jax.random.normal(ks[1], (D_MODEL, D_MODEL), dtype=jnp.float32) * s, 'Wk1': jax.random.normal(ks[2], (D_MODEL, D_MODEL), dtype=jnp.float32) * s, 'Wk2': jax.random.normal(ks[3], (D_MODEL, D_MODEL), dtype=jnp.float32) * s, 'Wv': jax.random.normal(ks[4], (D_MODEL, D_MODEL), dtype=jnp.float32) * s, 'Wo': jax.random.normal(ks[5], (D_MODEL, D_MODEL), dtype=jnp.float32) * s, 'lambda_logit': jnp.zeros((N_HEADS,), dtype=jnp.float32)}
    _L0_attn_in = _L0_attn_setup()

    def _L0_ffn_setup():
        import jax, jax.numpy as jnp
        import numpy as np
        B, S, H, F, E = (4, 256, 128, 512, 8)
        key = jax.random.key(seed)
        ks = jax.random.split(key, 8)
        s = 1.0 / np.sqrt(H)
        sf = 1.0 / np.sqrt(F)
        return {'x': jax.random.normal(ks[0], (B, S, H), jnp.float32), 'wr': jax.random.uniform(ks[1], (H, E), jnp.float32, -s, s), 'br': jax.random.uniform(ks[2], (E,), jnp.float32, -s, s), 'w1': jax.random.uniform(ks[3], (E, H, F), jnp.float32, -s, s), 'b1': jax.random.uniform(ks[4], (E, F), jnp.float32, -s, s), 'w2': jax.random.uniform(ks[5], (E, F, H), jnp.float32, -sf, sf), 'b2': jax.random.uniform(ks[6], (E, H), jnp.float32, -sf, sf)}
    _L0_ffn_in = _L0_ffn_setup()
    _d = {'L0_attn_x': _L0_attn_in['x'], 'L0_attn_Wq': _L0_attn_in['Wq'], 'L0_attn_Wk1': _L0_attn_in['Wk1'], 'L0_attn_Wk2': _L0_attn_in['Wk2'], 'L0_attn_Wv': _L0_attn_in['Wv'], 'L0_attn_Wo': _L0_attn_in['Wo'], 'L0_attn_lambda_logit': _L0_attn_in['lambda_logit'], 'L0_ffn_wr': _L0_ffn_in['wr'], 'L0_ffn_br': _L0_ffn_in['br'], 'L0_ffn_w1': _L0_ffn_in['w1'], 'L0_ffn_b1': _L0_ffn_in['b1'], 'L0_ffn_w2': _L0_ffn_in['w2'], 'L0_ffn_b2': _L0_ffn_in['b2']}
    _x0 = _d['L0_attn_x']
    _d['L0_attn_x'] = jax.random.normal(jax.random.fold_in(jax.random.key(seed), 1), (4, 512, 128), dtype=_x0.dtype)
    del _x0
    return _d

def reference(L0_attn_x, L0_attn_Wq, L0_attn_Wk1, L0_attn_Wk2, L0_attn_Wv, L0_attn_Wo, L0_attn_lambda_logit, L0_ffn_wr, L0_ffn_br, L0_ffn_w1, L0_ffn_b1, L0_ffn_w2, L0_ffn_b2):

    def _L0_attn_ref(x, Wq, Wk1, Wk2, Wv, Wo, lambda_logit):
        import jax, jax.numpy as jnp
        import numpy as np
        D_MODEL = 128
        N_HEADS = 16
        HEAD_DIM = D_MODEL // N_HEADS
        SCALE = HEAD_DIM ** (-0.5)
        MIN_VAL = jnp.finfo(jnp.float32).min

        def _split_heads(y):
            B, T, _ = y.shape
            return y.reshape(B, T, N_HEADS, HEAD_DIM).transpose(0, 2, 1, 3)
        B, T, _ = x.shape
        q = _split_heads(x @ Wq.T)
        k1 = _split_heads(x @ Wk1.T)
        k2 = _split_heads(x @ Wk2.T)
        v = _split_heads(x @ Wv.T)
        s1 = jnp.einsum('bhqd,bhkd->bhqk', q, k1) * SCALE
        s2 = jnp.einsum('bhqd,bhkd->bhqk', q, k2) * SCALE
        causal = jnp.arange(T)[None, :] <= jnp.arange(T)[:, None]
        s1 = jnp.where(causal[None, None], s1, MIN_VAL)
        s2 = jnp.where(causal[None, None], s2, MIN_VAL)
        attn_exp = jax.nn.softmax(s1, axis=-1)
        attn_noise = jax.nn.softmax(s2, axis=-1)
        lam = jax.nn.sigmoid(lambda_logit)[None, :, None, None]
        attn = attn_exp - lam * attn_noise
        denom = jnp.maximum(jnp.sum(jnp.abs(attn), axis=-1, keepdims=True), 1e-06)
        attn = attn / denom
        out = jnp.einsum('bhqk,bhkd->bhqd', attn, v)
        out = out.transpose(0, 2, 1, 3).reshape(B, T, D_MODEL)
        return out @ Wo.T

    def _L0_ffn_ref(x, wr, br, w1, b1, w2, b2):
        import jax, jax.numpy as jnp
        import numpy as np
        B, S, H, F, E = (4, 256, 128, 512, 8)
        scores = jnp.einsum('bsh,he->bse', x, wr) + br
        expert_id = jnp.argmax(scores, axis=-1)
        h = jnp.einsum('bsh,ehf->ebsf', x, w1) + b1[:, None, None, :]
        h = jax.nn.gelu(h, approximate=False)
        y = jnp.einsum('ebsf,efh->ebsh', h, w2) + b2[:, None, None, :]
        one_hot = jax.nn.one_hot(expert_id, E, dtype=x.dtype)
        out = jnp.einsum('ebsh,bse->bsh', y, one_hot)
        return out
    x = L0_attn_x
    x = x + 0.5 * _L0_ffn_ref(_layernorm(x, axis=-1), L0_ffn_wr, L0_ffn_br, L0_ffn_w1, L0_ffn_b1, L0_ffn_w2, L0_ffn_b2)
    x = x + _L0_attn_ref(_layernorm(x, axis=-1), L0_attn_Wq, L0_attn_Wk1, L0_attn_Wk2, L0_attn_Wv, L0_attn_Wo, L0_attn_lambda_logit)
    x = x + 0.5 * _L0_ffn_ref(_layernorm(x, axis=-1), L0_ffn_wr, L0_ffn_br, L0_ffn_w1, L0_ffn_b1, L0_ffn_w2, L0_ffn_b2)
    return x

_drawn_inputs = setup_inputs


def setup_inputs(seed=0):
    import zlib

    import numpy as np

    out = dict(_drawn_inputs(seed))
    spreads = {'L0_attn_lambda_logit': (0.0, 0.612)}
    factors = {'L0_ffn_b1': 2.761}
    for name, (base, spread) in spreads.items():
        noise = np.random.default_rng([zlib.crc32(name.encode()), seed]).standard_normal(out[name].shape)
        drawn = base * np.exp(spread * noise) if base else spread * noise
        out[name] = jnp.asarray(drawn.astype(out[name].dtype))
    for name, factor in factors.items():
        out[name] = (out[name] * factor).astype(out[name].dtype)
    return out
```

```python
from contextlib import ExitStack

import concourse.bass as bass
from concourse import mybir

ALU = mybir.AluOpType
ACT = mybir.ActivationFunctionType
AX = mybir.AxisListType
F32 = mybir.dt.float32
BF16 = mybir.dt.bfloat16
I32 = mybir.dt.int32
U32 = mybir.dt.uint32

P = 128
BATCH, SEQ, D = 4, 512, 128
NBLK = BATCH * SEQ // P
BPB = SEQ // P
HEADS, HD = 16, 8
E, F = 8, 512
FC = F // P
LN_EPS = 1e-5
SCALE = HD ** -0.5
DENOM_MIN = 1e-6
MASKED = -3.0e38

REGION = BATCH * SEQ + P
TILES = NBLK + E - 1
SPARE = E * REGION

Q_PARTS = [0, 0, 0, 1, 1, 2]
K_PARTS = [0, 1, 2, 0, 1, 0]
TERMS = len(Q_PARTS)
ROWS = TERMS * HD
QUADS = HEADS // 4

GROUPS_OF_QUAD = ([(3, [a]) for a in range(4)] + [(2, [a]) for a in range(4)]
                  + [(1, [0, 1]), (1, [2, 3])] + [(0, [0, 1, 2, 3])])
GPQ = len(GROUPS_OF_QUAD)
GROUPS = [(quad, i, heads) for quad in range(QUADS) for i, heads in GROUPS_OF_QUAD]
NG = len(GROUPS)


def nth(per, it, n):
    return it * per + (n + 1)


def build(nc, x, wq, wk1, wk2, wv, wo, lam, wr, br, w1, b1, w2, b2, out):
    with ExitStack() as ctx:
        def sb(name, shape, dt=F32):
            return ctx.enter_context(nc.sbuf_tensor(name, shape, dt))

        def sem(name):
            return ctx.enter_context(nc.semaphore(name))

        bank = [ctx.enter_context(nc.psum_tensor(f"bank{i}", [P, 512], F32)) for i in range(8)]

        X = sb("X", [P, NBLK, D])
        W1 = sb("W1", [P, E * F])
        W2 = sb("W2", [P, E * FC * D])
        WT = sb("WT", [P, 5, D])
        wraw = sb("wraw", [P, 5, D])
        wr_sb = sb("wr_sb", [P, E])
        br_sb = sb("br_sb", [1, E])
        B1S = sb("B1S", [3, E * F], BF16)
        B2S = sb("B2S", [3, E * D], BF16)
        ident = sb("ident", [P, P])
        identb = sb("identb", [P, P], BF16)
        maskb = sb("maskb", [P, P], BF16)
        trib = sb("trib", [P, P], BF16)
        onesb = sb("onesb", [P, P], BF16)
        ones1 = sb("ones1", [1, P])
        zeros = sb("zeros", [P, D])
        mhalf = sb("mhalf", [P, BPB])
        nlam = sb("nlam", [P, HEADS])
        lamt = sb("lamt", [P, 2, HEADS])
        em8 = sb("em8", [P, E])
        ereg = sb("ereg", [P, E])
        tri8 = sb("tri8", [P, E, E])
        iot = sb("iot", [P, TILES])
        iot128 = sb("iot128", [P, TILES])
        e9 = sb("e9", [P, E + 1])
        braw = sb("braw", [P, E * F // P + E * D // P])
        bres = sb("bres", [P, 2, E * F // P + E * D // P])
        bpart = sb("bpart", [P, 3, E * F // P + E * D // P], BF16)

        stats = sb("stats", [P, 2, BPB, 6])
        mv = sb("mv", [P, 2, BPB, 2])
        veps = sb("veps", [P, 2, BPB])
        rstd = sb("rstd", [P, 2, BPB])
        xn = sb("xn", [P, 2, BPB, D])
        xnT = sb("xnT", [P, 2, SEQ])
        rmax = sb("rmax", [P, 2, BPB])
        req = sb("req", [P, 2, BPB, E])
        rcand = sb("rcand", [P, 2, BPB, E])
        rmin = sb("rmin", [P, 2, BPB])
        OH = sb("OH", [P, NBLK, E], BF16)
        seen = sb("seen", [P, E], BF16)
        seenf = sb("seenf", [P, 2, E])
        place = sb("place", [P, 2, BPB, E])
        SLOT = sb("SLOT", [P, NBLK])
        slotu = sb("slotu", [P, 2, BPB], U32)
        cnt = sb("cnt", [P, E])
        cnti = sb("cnti", [P, E], I32)
        ntile = sb("ntile", [P, E])
        ntilei = sb("ntilei", [P, E], I32)
        cprod = sb("cprod", [P, E, E])
        cend = sb("cend", [P, E])
        cstart = sb("cstart", [P, E])
        shift = sb("shift", [P, E])
        tge = sb("tge", [P, TILES, E])
        texp = sb("texp", [P, TILES])
        tone = sb("tone", [P, TILES, E + 1])
        trow = sb("trow", [P, TILES, E + 1])
        trowf = sb("trowf", [P, TILES])
        tilee = sb("tilee", [P, TILES], I32)
        tiler = sb("tiler", [P, TILES], I32)
        yprod = sb("yprod", [P, NBLK, E])
        ysub = sb("ysub", [P, NBLK])
        yslot = sb("yslot", [P, NBLK], U32)
        YG = sb("YG", [P, NBLK, D])

        tin = sb("tin", [P, 2, D])
        tinT = sb("tinT", [P, 2, P])
        hid = sb("hid", [P, 2, F])
        hidT = sb("hidT", [P, 2, FC, P])
        ytile = sb("ytile", [P, 2, D])

        V = sb("V", [P, NBLK, D])
        parts = sb("parts", [P, 2, 3, 3, SEQ], BF16)
        resid = sb("resid", [P, 3, SEQ])
        stack = sb("stack", [P, 2, 3, 2, SEQ], BF16)
        negm = sb("negm", [P, 2, 8])
        ex = sb("ex", [P, 2, 1024])
        w = sb("w", [P, 2, 512])
        wT = sb("wT", [P, 2, 512])
        Z = sb("Z", [P, 2, 16, 2])
        rz2 = sb("rz2", [P, 2, 4])
        ratio = sb("ratio", [P, 2, 4])
        coef = sb("coef", [P, 2, 4])
        asum = sb("asum", [P, 2, 16])
        den = sb("den", [P, 2, 16])
        rden = sb("rden", [P, 2, 16])
        vq = sb("vq", [P, 2, BPB, 32])
        ob = sb("ob", [P, BPB, D])
        obT = sb("obT", [P, SEQ])

        XS = nc.dram_tensor("rows_by_expert", [SPARE + P, D], F32, kind="Internal").ap()
        YS = nc.dram_tensor("rows_by_tile", [TILES * P, D], F32, kind="Internal").ap()
        KD = nc.dram_tensor("stacks", [3, BATCH, QUADS * 2, ROWS * 2, SEQ], BF16, kind="Internal").ap()

        x_in = sem("x_in")
        small_in = sem("small_in")
        w1_in = sem("w1_in")
        w2_in = sem("w2_in")
        pool_set = sem("pool_set")
        dve_set = sem("dve_set")
        act_set = sem("act_set")
        pe_set = sem("pe_set")
        bias_in = sem("bias_in")
        spare_zero = sem("spare_zero")
        out_stored = sem("out_stored")

        NSET_POOL = 17

        def setup_sp(sp):
            sp.dma_start(X[:], x.rearrange("b (t p) d -> p (b t) d", p=P)).then_inc(x_in, 16)
            for t, src in enumerate((wq, wk1, wk2, wv, wo)):
                sp.dma_start(wraw[:, t, :], src).then_inc(small_in, 16)
            sp.dma_start(wr_sb[:], wr).then_inc(small_in, 16)
            sp.dma_start(br_sb[:], br.rearrange("(a e) -> a e", a=1)).then_inc(small_in, 16)
            sp.dma_start(lamt[:, 0, :], lam.rearrange("(a e) -> a e", a=1).to_broadcast([P, HEADS])).then_inc(small_in, 16)
            sp.dma_start(braw[:, 0:E * F // P], b1.rearrange("e (a f) -> (e a) f", a=P // E)).then_inc(small_in, 16)
            sp.dma_start(braw[:, E * F // P:], b2.rearrange("e (a f) -> (e a) f", a=P // E)).then_inc(small_in, 16)
            sp.dma_start(W1[:].rearrange("p (e f) -> p e f", e=E), w1.rearrange("e h f -> h e f")).then_inc(w1_in, 16)
            sp.dma_start(W2[:].rearrange("p (e c h) -> p e c h", e=E, c=FC),
                         w2.rearrange("e (c p) h -> p e c h", p=P)).then_inc(w2_in, 16)
            sp.wait_ge(dve_set, 4 + 5)
            for k in range(3):
                sp.dma_start(B1S[k:k + 1, :], bpart[:, k, 0:E * F // P]).then_inc(bias_in, 16)
                sp.dma_start(B2S[k:k + 1, :], bpart[:, k, E * F // P:]).then_inc(bias_in, 16)
            sp.wait_ge(pool_set, NSET_POOL)
            sp.dma_start(XS[SPARE:SPARE + P, :], zeros[:]).then_inc(spare_zero, 16)

        def setup_pool(pool):
            n = [0]

            def step(ins):
                n[0] += 1
                return ins.then_inc(pool_set, 1)

            step(pool.memset(ident[:], 0.0))
            step(pool.memset(maskb[:], 0.0))
            step(pool.memset(onesb[:], 1.0))
            step(pool.memset(tri8[:], 1.0))
            step(pool.memset(zeros[:], 0.0))
            step(pool.memset(mhalf[:], -0.5))
            step(pool.memset(ones1[:], 1.0))
            step(pool.memset(seen[:], 0.0))
            pool.wait_ge(pool_set, n[0])
            step(pool.affine_select(out=ident[:], in_=ident[:], compare_op=ALU.not_equal, fill=1.0, base=0,
                                    pattern=[[-1, P]], channel_multiplier=1))
            step(pool.affine_select(out=maskb[:], in_=maskb[:], compare_op=ALU.is_ge, fill=MASKED, base=0,
                                    pattern=[[-1, P]], channel_multiplier=1))
            step(pool.affine_select(out=trib[:], in_=onesb[:], compare_op=ALU.is_gt, fill=0.0, base=0,
                                    pattern=[[1, P]], channel_multiplier=-1))
            step(pool.affine_select(out=tri8[:], in_=tri8[:], compare_op=ALU.is_ge, fill=0.0, base=0,
                                    pattern=[[1, E], [-1, E]], channel_multiplier=0))
            for t, base, k, m in ((em8, -8, 1, E), (ereg, 0, REGION, E), (e9, 0, 1, E + 1), (iot, 0, 1, TILES),
                                  (iot128, 0, P, TILES)):
                step(pool.iota(t[:], pattern=[[k, m]], base=base, channel_multiplier=0,
                               allow_small_or_imprecise_dtypes=True))
            assert n[0] == NSET_POOL

        def setup_dve(v):
            v.wait_ge(small_in, 16 * 10)
            v.tensor_copy(bpart[:, 0, :], braw[:]).then_inc(dve_set, 1)
            v.wait_ge(dve_set, 1)
            v.tensor_tensor(bres[:, 0, :], braw[:], bpart[:, 0, :], ALU.subtract).then_inc(dve_set, 1)
            v.wait_ge(dve_set, 2)
            v.tensor_copy(bpart[:, 1, :], bres[:, 0, :]).then_inc(dve_set, 1)
            v.wait_ge(dve_set, 3)
            v.tensor_tensor(bpart[:, 2, :], bres[:, 0, :], bpart[:, 1, :], ALU.subtract).then_inc(dve_set, 1)
            v.wait_ge(pool_set, NSET_POOL)
            v.tensor_copy(identb[:], ident[:]).then_inc(dve_set, 1)
            v.wait_ge(act_set, 1)
            v.tensor_scalar(lamt[:, 0, :], lamt[:, 1, :], 1.0, -1.0, ALU.add, ALU.mult).then_inc(dve_set, 1)
            v.wait_ge(dve_set, 6)
            v.reciprocal(nlam[:], lamt[:, 0, :]).then_inc(dve_set, 1)
            v.memset(trow[:, :, E:E + 1], float(SPARE)).then_inc(dve_set, 1)
            v.wait_ge(pe_set, 1)
            for t in range(3):
                v.tensor_copy(WT[:, t, :].rearrange("k (g d h) -> k g d h", h=2, d=HD),
                              bank[0][:, t * D:(t + 1) * D].rearrange("k (g h d) -> k g d h", h=2, d=HD)).then_inc(dve_set, 1)
            v.tensor_copy(WT[:, 3, :], bank[0][:, 3 * D:4 * D]).then_inc(dve_set, 1)
            v.tensor_copy(WT[:, 4, :], bank[1][:, 0:D]).then_inc(dve_set, 1)

        def setup_act(a):
            a.wait_ge(small_in, 16 * 10)
            a.activation(lamt[:, 1, :], lamt[:, 0, :], ACT.Exp, scale=-1.0).then_inc(act_set, 1)

        def setup_pe(pe):
            pe.wait_ge(small_in, 16 * 10)
            pe.wait_ge(pool_set, NSET_POOL)
            for t in range(5):
                last = pe.transpose(bank[t // 4][:, (t % 4) * D:(t % 4 + 1) * D], wraw[:, t, :], ident[:])
            last.then_inc(pe_set, 1)

        DVE_SET = 13

        class Norm:

            def __init__(self, tag):
                self.stat = sem(f"{tag}_stat")
                self.mv = sem(f"{tag}_mv")
                self.veps = sem(f"{tag}_veps")
                self.rstd = sem(f"{tag}_rstd")
                self.xn = sem(f"{tag}_xn")
                self.tr = sem(f"{tag}_tr")
                self.xnT = sem(f"{tag}_xnT")

            def dve_stats(self, v, b, s):
                for j in range(BPB):
                    v.bn_stats(stats[:, s, j, :], X[:, bass.ds(b * BPB + j, 1), :]).then_inc(self.stat, 1)
                v.wait_ge(self.stat, (b + 1) * BPB)
                for j in range(BPB):
                    ins = v.bn_aggr(mv[:, s, j, :], stats[:, s, j, :])
                ins.then_inc(self.mv, 1)

            def pool(self, pool, b, s):
                pool.wait_ge(self.mv, b + 1)
                pool.tensor_scalar(veps[:, s, :], mv[:, s, :, 1], LN_EPS, None, ALU.add).then_inc(self.veps, 1)
                pool.wait_ge(self.veps, b + 1)
                pool.tensor_tensor(rstd[:, s, :], veps[:, s, :], mhalf[:], ALU.pow).then_inc(self.rstd, 1)

            def dve_apply(self, v, b, s):
                v.wait_ge(self.rstd, b + 1)
                for j in range(BPB):
                    ins = v.tensor_scalar(xn[:, s, j, :], X[:, bass.ds(b * BPB + j, 1), :], mv[:, s, j, 0:1],
                                          rstd[:, s, j:j + 1], ALU.subtract, ALU.mult)
                ins.then_inc(self.xn, 1)

            def pe(self, pe, b, s):
                pe.wait_ge(self.xn, b + 1)
                for j in range(BPB):
                    ins = pe.transpose(bank[s][:, j * P:(j + 1) * P], xn[:, s, j, :], ident[:])
                ins.then_inc(self.tr, 1)

            def act(self, a, b, s):
                a.wait_ge(self.tr, b + 1)
                a.copy(xnT[:, s, :], bank[s][:]).then_inc(self.xnT, 1)

        def ffn(tag, before, store):
            norm = Norm(tag)
            score = sem(f"{tag}_score")
            rmax_d = sem(f"{tag}_rmax")
            req_d = sem(f"{tag}_req")
            cand_d = sem(f"{tag}_cand")
            rmin_d = sem(f"{tag}_rmin")
            oh_d = sem(f"{tag}_oh")
            rank = sem(f"{tag}_rank")
            sum_d = sem(f"{tag}_sum")
            seen_d = sem(f"{tag}_seen")
            place_d = sem(f"{tag}_place")
            slot_d = sem(f"{tag}_slot")
            scattered = [sem(f"{tag}_scattered{s}") for s in range(2)]
            count_p = sem(f"{tag}_count")
            table = sem(f"{tag}_table")
            padded = sem(f"{tag}_padded")
            tin_in = [sem(f"{tag}_tin{s}") for s in range(2)]
            tinT_p = sem(f"{tag}_tinT_p")
            tinT_d = sem(f"{tag}_tinT")
            hid_p = sem(f"{tag}_hid_p")
            hid_d = sem(f"{tag}_hid")
            hidT_p = sem(f"{tag}_hidT_p")
            hidT_d = sem(f"{tag}_hidT")
            y_p = sem(f"{tag}_y_p")
            y_d = sem(f"{tag}_y")
            y_out = [sem(f"{tag}_y_out{s}") for s in range(2)]
            gathered = [sem(f"{tag}_gathered{b}") for b in range(BATCH)]
            x_d = sem(f"{tag}_x")

            def route_dve(v, b, s):
                blocks = bass.ds(b * BPB, BPB)
                sc = bank[2 + s][:, 0:BPB * E].rearrange("p (j e) -> p j e", e=E)
                em8b = em8[:].rearrange("p (a e) -> p a e", a=1).to_broadcast([P, BPB, E])

                def over_e(t):
                    return t.rearrange("p (j a) -> p j a", a=1).to_broadcast([P, BPB, E])

                norm.dve_stats(v, b, s)
                if not (isinstance(b, int) and b < 2):
                    v.wait_ge(scattered[s], (b - s) * (8 * BPB))
                norm.dve_apply(v, b, s)
                v.wait_ge(score, b + 1)
                v.tensor_reduce(rmax[:, s, :], sc, AX.X, ALU.max).then_inc(rmax_d, 1)
                v.wait_ge(rmax_d, b + 1)
                v.tensor_tensor(req[:, s], sc, over_e(rmax[:, s, :]), ALU.is_equal).then_inc(req_d, 1)
                v.wait_ge(req_d, b + 1)
                v.tensor_tensor(rcand[:, s], req[:, s], em8b, ALU.mult).then_inc(cand_d, 1)
                v.wait_ge(cand_d, b + 1)
                v.tensor_reduce(rmin[:, s, :], rcand[:, s], AX.X, ALU.min).then_inc(rmin_d, 1)
                v.wait_ge(rmin_d, b + 1)
                v.tensor_tensor(OH[:, blocks, :], em8b, over_e(rmin[:, s, :]), ALU.is_equal).then_inc(oh_d, 1)
                v.wait_ge(oh_d, b + 1)
                v.tensor_reduce(seenf[:, s, :], OH[:, blocks, :].rearrange("p j e -> p e j"), AX.X, ALU.add).then_inc(sum_d, 1)
                v.wait_ge(rank, b + 1)
                v.tensor_tensor(place[:, s], bank[4 + s][:, 0:BPB * E].rearrange("p (j e) -> p j e", e=E),
                                ereg[:].rearrange("p (a e) -> p a e", a=1).to_broadcast([P, BPB, E]), ALU.add).then_inc(place_d, 1)
                v.wait_ge(sum_d, b + 1)
                v.tensor_tensor(seen[:], seen[:], seenf[:, s, :], ALU.add).then_inc(seen_d, 1)
                v.wait_ge(place_d, 2 * b + 1)
                v.tensor_tensor(place[:, s], place[:, s], OH[:, blocks, :], ALU.mult).then_inc(place_d, 1)
                v.wait_ge(place_d, 2 * b + 2)
                v.tensor_reduce(SLOT[:, blocks], place[:, s], AX.X, ALU.add).then_inc(slot_d, 1)
                v.wait_ge(slot_d, 2 * b + 1)
                v.tensor_copy(slotu[:, s, :], SLOT[:, blocks]).then_inc(slot_d, 1)

            def route_pe(pe, b, s):
                norm.pe(pe, b, s)
                pe.wait_ge(norm.xnT, b + 1)
                for j in range(BPB):
                    o = bank[2 + s][:, j * E:(j + 1) * E]
                    pe.matmul(o, ones1[:], br_sb[:], start=True, stop=False)
                    ins = pe.matmul(o, xnT[:, s, j * P:(j + 1) * P], wr_sb[:], start=False, stop=True)
                ins.then_inc(score, 1)
                pe.wait_ge(oh_d, b + 1)
                if not (isinstance(b, int) and b == 0):
                    pe.wait_ge(seen_d, b)
                r = bank[4 + s][:, 0:BPB * E].rearrange("p (j e) -> p j e", e=E)
                pe.matmul(r, onesb[:], seen[:].rearrange("p (a e) -> p a e", a=1).to_broadcast([P, BPB, E]),
                          start=True, stop=False, skip_group_check=True)
                for j in range(BPB - 1):
                    pe.matmul(r[:, j + 1:, :], onesb[:], OH[:, bass.ds(b * BPB + j, 1), :].to_broadcast([P, BPB - 1 - j, E]),
                              start=False, stop=False, skip_group_check=True)
                for j in range(BPB):
                    ins = pe.matmul(r[:, j, :], trib[:], OH[:, bass.ds(b * BPB + j, 1), :],
                                    start=False, stop=j == BPB - 1, skip_group_check=True)
                ins.then_inc(rank, 1)

            def route_pool(pool, b, s):
                norm.pool(pool, b, s)
                pool.wait_ge(slot_d, 2 * b + 2)
                for j in range(BPB):
                    pool.indirect_dma_start(out=XS, out_offset=bass.IndirectOffsetOnAxis(ap=slotu[:, s, j:j + 1], axis=0),
                                            in_=xn[:, s, j, :], in_offset=None).then_inc(scattered[s], 16)

            def over_batches(eng, body):
                for b in range(2):
                    body(eng, b, b)
                with eng.Fori(1, BATCH // 2) as pair:
                    for s in range(2):
                        body(eng, pair * 2 + s, s)

            def table_dve(v):
                n = [0]

                def step(ins):
                    ins.then_inc(table, 1)
                    n[0] += 1
                    v.wait_ge(table, n[0])

                def mid(t, k, m):
                    return t.rearrange("p (a e) -> p a e", a=1).to_broadcast([P, k, m])

                def last(t, k, m):
                    return t.rearrange("p (j a) -> p j a", a=1).to_broadcast([P, k, m])

                v.wait_ge(count_p, 1)
                step(v.tensor_copy(cnt[:], bank[6][:, 0:E]))
                step(v.tensor_copy(cnti[:], cnt[:]))
                step(v.tensor_scalar(ntile[:], cnt[:], 1.0 / P, (P - 1) / (2.0 * P), ALU.mult, ALU.add))
                step(v.tensor_copy(ntilei[:], ntile[:]))
                step(v.tensor_copy(ntile[:], ntilei[:]))
                step(v.tensor_tensor(cprod[:], tri8[:], mid(ntile[:], E, E), ALU.mult))
                step(v.tensor_reduce(cend[:], cprod[:], AX.X, ALU.add))
                step(v.tensor_tensor(cstart[:], cend[:], ntile[:], ALU.subtract))
                step(v.scalar_tensor_tensor(out=shift[:], in0=cstart[:], scalar=-float(P), in1=ereg[:],
                                            op0=ALU.mult, op1=ALU.add))
                step(v.tensor_tensor(tge[:], last(iot[:], TILES, E), mid(cend[:], TILES, E), ALU.is_ge))
                step(v.tensor_reduce(texp[:], tge[:], AX.X, ALU.add))
                step(v.tensor_tensor(tone[:], last(texp[:], TILES, E + 1), mid(e9[:], TILES, E + 1), ALU.is_equal))
                step(v.tensor_tensor(trow[:, :, 0:E], last(iot128[:], TILES, E), mid(shift[:], TILES, E), ALU.add))
                step(v.tensor_tensor(tone[:], tone[:], trow[:], ALU.mult))
                step(v.tensor_reduce(trowf[:], tone[:], AX.X, ALU.add))
                step(v.tensor_copy(tiler[:], trowf[:]))
                step(v.tensor_scalar(tilee[:], texp[:], float(E - 1), None, ALU.min))
                step(v.tensor_tensor(yprod[:], OH[:], mid(shift[:], NBLK, E), ALU.mult))
                step(v.tensor_reduce(ysub[:], yprod[:], AX.X, ALU.add))
                step(v.tensor_tensor(yslot[:], SLOT[:], ysub[:], ALU.subtract))
                step(v.memset(seen[:], 0.0))
                assert n[0] == TABLE

            TABLE, TABLE_COUNTS, TABLE_TILES = 21, 2, 17

            def load_tile(sp, t, s):
                if not (isinstance(t, int) and t < 2):
                    sp.wait_ge(tinT_p, t - 1)
                row = sp.value_load(tiler[0:1, bass.ds(t, 1)], min_val=0, max_val=SPARE)
                sp.dma_start(tin[:, s, :], XS[bass.ds(row, P), :]).then_inc(tin_in[s], 16)

            def turn_in(pe, t, s):
                pe.wait_ge(tin_in[s], (t // 2 + 1) * 16 if isinstance(t, int) else (t - s) * 8 + 16)
                if not (isinstance(t, int) and t < 2):
                    pe.wait_ge(tinT_d, t - 1)
                pe.transpose(bank[s][:, 0:P], tin[:, s, :], ident[:]).then_inc(tinT_p, 1)

            def up(pe, t, s):
                e = pe.value_load(tilee[0:1, bass.ds(t, 1)], min_val=0, max_val=E - 1)
                pe.wait_ge(tinT_d, t + 1)
                if not (isinstance(t, int) and t < 2):
                    pe.wait_ge(hid_d, t - 1)
                pe.matmul(bank[2 + s][:], onesb[0:3, :], B1S[:, bass.ds(e * F, F)], start=True, stop=False)
                pe.matmul(bank[2 + s][:], tinT[:, s, :], W1[:, bass.ds(e * F, F)],
                          start=False, stop=True).then_inc(hid_p, 1)

            def turn_hidden(pe, t, s):
                pe.wait_ge(hid_d, t + 1)
                if not (isinstance(t, int) and t < 2):
                    pe.wait_ge(hidT_d, t - 1)
                for c in range(FC):
                    ins = pe.transpose(bank[4 + s][:, c * P:(c + 1) * P], hid[:, s, c * P:(c + 1) * P], ident[:])
                ins.then_inc(hidT_p, 1)

            def down(pe, t, s):
                e = pe.value_load(tilee[0:1, bass.ds(t, 1)], min_val=0, max_val=E - 1)
                pe.wait_ge(hidT_d, t + 1)
                if not (isinstance(t, int) and t < 2):
                    pe.wait_ge(y_d, t - 1)
                pe.matmul(bank[6 + s][:, 0:D], onesb[0:3, :], B2S[:, bass.ds(e * D, D)], start=True, stop=False)
                for c in range(FC):
                    ins = pe.matmul(bank[6 + s][:, 0:D], hidT[:, s, c, :], W2[:, bass.ds(e * (FC * D) + c * D, D)],
                                    start=False, stop=c == FC - 1)
                ins.then_inc(y_p, 1)

            def over_tiles(eng, step):
                for t in range(4):
                    step(eng, t, t % 2)
                with eng.Fori(2, (TILES - 1) // 2) as pair:
                    for s in range(2):
                        step(eng, pair * 2 + s, s)
                for t in range(TILES - 1, TILES + 2):
                    step(eng, t, t % 2)

            def known(t, lo, hi):
                return not isinstance(t, int) or lo <= t < hi

            def tile_pe(pe, t, s):
                if known(t, 0, TILES):
                    up(pe, t, s)
                if known(t, 1, TILES + 1):
                    turn_hidden(pe, t - 1, 1 - s)
                if known(t, 0, TILES - 1):
                    turn_in(pe, t + 1, 1 - s)
                if known(t, 2, TILES + 2):
                    down(pe, t - 2, s)

            def tile_act(a, t, s):
                if known(t, 0, TILES):
                    a.wait_ge(hid_p, t + 1)
                    if not (isinstance(t, int) and t < 2):
                        a.wait_ge(hidT_p, t - 1)
                    a.activation(hid[:, s, :], bank[2 + s][:], ACT.Gelu).then_inc(hid_d, 1)
                if known(t, 2, TILES + 2):
                    a.wait_ge(y_p, t - 1)
                    if not (isinstance(t, int) and t < 4):
                        a.wait_ge(y_out[s], (t // 2 - 1) * 16 if isinstance(t, int) else (t - s) * 8 - 16)
                    a.copy(ytile[:, s, :], bank[6 + s][:, 0:D]).then_inc(y_d, 1)
                    a.wait_ge(y_d, t - 1)
                    a.dma_start(YS[bass.ds((t - 2) * P, P), :], ytile[:, s, :]).then_inc(y_out[s], 16)

            def tile_dve(v, t, s):
                if known(t, 1, TILES + 1):
                    v.wait_ge(hidT_p, t)
                    if not (isinstance(t, int) and t < 3):
                        v.wait_ge(y_p, t - 2)
                    v.tensor_copy(hidT[:, 1 - s].rearrange("p c k -> p (c k)"), bank[4 + 1 - s][:]).then_inc(hidT_d, 1)
                if known(t, 0, TILES - 1):
                    v.wait_ge(tinT_p, t + 2)
                    if not (isinstance(t, int) and t < 1):
                        v.wait_ge(hid_p, t)
                    v.tensor_copy(tinT[:, 1 - s, :], bank[1 - s][:, 0:P]).then_inc(tinT_d, 1)

            def sp_part(sp):
                sp.wait_ge(table, TABLE_COUNTS)
                for e in range(E):
                    n = sp.value_load(cnti[0:1, e:e + 1], min_val=0, max_val=BATCH * SEQ)
                    sp.dma_start(XS[bass.ds(n + e * REGION, P), :], zeros[:]).then_inc(padded, 16)
                sp.wait_ge(table, TABLE_TILES)
                sp.wait_ge(padded, 16 * E)
                sp.wait_ge(spare_zero, 16)
                for s in range(2):
                    sp.wait_ge(scattered[s], 16 * NBLK // 2)
                for t in range(2):
                    load_tile(sp, t, t)
                with sp.Fori(1, (TILES - 1) // 2) as pair:
                    for s in range(2):
                        load_tile(sp, pair * 2 + s, s)
                load_tile(sp, TILES - 1, (TILES - 1) % 2)
                if store:
                    for b in range(BATCH):
                        sp.wait_ge(x_d, b + 1)
                        sp.dma_start(out[b].rearrange("(t p) d -> p t d", p=P), X[:, b * BPB:(b + 1) * BPB, :]).then_inc(out_stored, 16)
                    sp.wait_ge(out_stored, 16 * BATCH)

            def pool_part(pool):
                over_batches(pool, route_pool)
                pool.wait_ge(table, TABLE)
                for s in range(2):
                    pool.wait_ge(y_out[s], 16 * ((TILES + 1 - s) // 2))
                for t in range(NBLK):
                    pool.indirect_dma_start(out=YG[:, t, :], out_offset=None, in_=YS,
                                            in_offset=bass.IndirectOffsetOnAxis(ap=yslot[:, t:t + 1], axis=0)).then_inc(gathered[t // BPB], 16)

            def dve_part(v):
                before(v)
                over_batches(v, route_dve)
                table_dve(v)
                v.wait_ge(tinT_p, 1)
                v.tensor_copy(tinT[:, 0, :], bank[0][:, 0:P]).then_inc(tinT_d, 1)
                over_tiles(v, tile_dve)
                for b in range(BATCH):
                    v.wait_ge(gathered[b], 16 * BPB)
                    xb = X[:, b * BPB:(b + 1) * BPB, :]
                    v.scalar_tensor_tensor(out=xb, in0=YG[:, b * BPB:(b + 1) * BPB, :], scalar=0.5, in1=xb,
                                           op0=ALU.mult, op1=ALU.add).then_inc(x_d, 1)

            def act_part(a):
                over_batches(a, norm.act)
                over_tiles(a, tile_act)

            def pe_part(pe):
                over_batches(pe, route_pe)
                pe.wait_ge(seen_d, BATCH)
                pe.matmul(bank[6][:, 0:E], onesb[:], seen[:], start=True, stop=True).then_inc(count_p, 1)
                pe.wait_ge(table, TABLE_TILES)
                pe.wait_ge(w1_in, 16)
                pe.wait_ge(w2_in, 16)
                pe.wait_ge(bias_in, 16 * 6)
                turn_in(pe, 0, 0)
                over_tiles(pe, tile_pe)

            return dict(sp=sp_part, pool=pool_part, dve=dve_part, act=act_part, pe=pe_part), x_d

        def attention(x_ready):
            norm = Norm("at")
            proj = sem("at_proj")
            vproj = sem("at_vproj")
            high = sem("at_high")
            res1 = sem("at_res1")
            middle = sem("at_middle")
            low = sem("at_low")
            v_d = sem("at_v")
            kd_out = [sem(f"at_kd_out{s}") for s in range(2)]
            loaded = [sem(f"at_loaded{s}") for s in range(2)]
            scored = sem("at_scored")
            maxed = sem("at_maxed")
            exped = sem("at_exped")
            rz_d = sem("at_rz")
            ratio_d = sem("at_ratio")
            coef_d = sem("at_coef")
            w_d = sem("at_w")
            asum_d = sem("at_asum")
            turned = sem("at_turned")
            wT_d = sem("at_wT")
            av_d = sem("at_av")
            vq_d = sem("at_vq")
            den_d = sem("at_den")
            rden_d = sem("at_rden")
            ob_d = sem("at_ob")
            obT_p = sem("at_obT_p")
            obT_d = sem("at_obT")
            op_p = sem("at_op_p")
            x_d = sem("at_x")

            def over_batches(eng, body):
                for b in range(2):
                    body(eng, b, b)
                with eng.Fori(1, BATCH // 2) as pair:
                    for s in range(2):
                        body(eng, pair * 2 + s, s)

            def late(b, k):
                return not (isinstance(b, int) and b < k)

            scales = (SCALE, 1.0, 1.0)

            def proj_dve(v, b, s):
                norm.dve_stats(v, b, s)
                if late(b, 2):
                    v.wait_ge(norm.tr, b - 1)
                norm.dve_apply(v, b, s)
                for t in range(3):
                    v.wait_ge(high, 3 * b + (t + 1))
                    if late(b, 1):
                        v.wait_ge(middle, 3 * b + (t - 2))
                    v.scalar_tensor_tensor(out=resid[:, t, :], in0=bank[2 + t][:], scalar=scales[t], in1=parts[:, s, t, 0, :],
                                           op0=ALU.mult, op1=ALU.subtract).then_inc(res1, 1)
                for t in range(3):
                    v.wait_ge(middle, 3 * b + (t + 1))
                    v.tensor_tensor(parts[:, s, t, 2, :], resid[:, t, :], parts[:, s, t, 1, :], ALU.subtract).then_inc(low, 1)

            def proj_pe(pe, b, s):
                norm.pe(pe, b, s)
                pe.wait_ge(norm.xnT, b + 1)
                for t in range(3):
                    if late(b, 1):
                        pe.wait_ge(res1, 3 * b + (t - 2))
                    pe.matmul(bank[2 + t][:], WT[:, t, :], xnT[:, s, :], start=True, stop=True).then_inc(proj, 1)
                if late(b, 1):
                    pe.wait_ge(v_d, b)
                for j in range(BPB):
                    ins = pe.matmul(bank[5][:, j * P:(j + 1) * P], xnT[:, s, j * P:(j + 1) * P], WT[:, 3, :], start=True, stop=True)
                ins.then_inc(vproj, 1)

            def proj_act(a, b, s):
                norm.act(a, b, s)
                if late(b, 2):
                    a.wait_ge(kd_out[s], (b - s) * (8 * 3 * TERMS))
                for t in range(3):
                    a.wait_ge(proj, 3 * b + (t + 1))
                    a.mul(parts[:, s, t, 0, :], bank[2 + t][:], scales[t]).then_inc(high, 1)
                a.wait_ge(vproj, b + 1)
                a.copy(V[:, bass.ds(b * BPB, BPB), :], bank[5][:].rearrange("p (j d) -> p j d", d=D)).then_inc(v_d, 1)
                for t in range(3):
                    a.wait_ge(res1, 3 * b + (t + 1))
                    a.copy(parts[:, s, t, 1, :], resid[:, t, :]).then_inc(middle, 1)

            def proj_sp(sp, b, s):
                sp.wait_ge(low, 3 * b + 3)
                for t in range(3):
                    for term, part in enumerate(Q_PARTS if t == 0 else K_PARTS):
                        sp.dma_start(KD[t, bass.ds(b, 1), :, term * 2 * HD:(term + 1) * 2 * HD, :],
                                     parts[:, s, t, part, :]).then_inc(kd_out[s], 16)

            def spot(i, k, st):
                return (2 * k + st) * (i + 1) * P if i < 2 else st * 512

            def s_ap(n, i, k, st, lo=0, hi=None):
                width = (i + 1) * P
                at = spot(i, k, st)
                b = bank[2 * (n % 2) + at // 512]
                return b[:, at % 512 + lo:at % 512 + (width if hi is None else hi)]

            def ex_ap(n, i, k, st):
                return ex[:, n % 2, spot(i, k, st):spot(i, k, st) + (i + 1) * P]

            def scores_pe(pe, it, n, first):
                quad, i, heads = GROUPS[n]
                slot = quad % 2
                if n % GPQ == 0:
                    pe.wait_ge(loaded[slot], (it * 2 + quad // 2 + 1) * (6 * 16))
                if not (first and n < 2):
                    pe.wait_ge(exped, nth(NG, it, n - 2))
                per_bank = (2 if i == 1 else 4) if i < 2 else 1
                for h in range(2):
                    o = bank[2 * (n % 2) + h][:, 0:per_bank * (i + 1) * P].rearrange("p (m c) -> p m c", m=per_bank)[:, :, i * P:]
                    pe.matmul(o, identb[:], maskb[:].rearrange("p (a c) -> p a c", a=1).to_broadcast([P, per_bank, P]),
                              start=True, stop=False, skip_group_check=True)
                for k, a in enumerate(heads):
                    r = slice(64 * (a // 2), 64 * (a // 2) + ROWS)
                    for st in range(2):
                        ins = pe.matmul(s_ap(n, i, k, st), stack[r, slot, 0, a % 2, i * P:(i + 1) * P],
                                        stack[r, slot, 1 + st, a % 2, 0:(i + 1) * P],
                                        start=False, stop=True, skip_group_check=True)
                ins.then_inc(scored, 1)

            def turn_pe(pe, it, n, first):
                _, i, heads = GROUPS[n % NG]
                pe.wait_ge(w_d, nth(NG, it, n))
                if not (first and n < 2):
                    pe.wait_ge(wT_d, nth(NG, it, n - 2))
                for c in range(len(heads) * (i + 1)):
                    ins = pe.transpose(bank[4 + n % 2][:, c * P:(c + 1) * P], w[:, n % 2, c * P:(c + 1) * P], ident[:])
                ins.then_inc(turned, 1)

            def av_pe(pe, it, n, first):
                quad, i, heads = GROUPS[n % NG]
                pe.wait_ge(wT_d, nth(NG, it, n))
                if n % GPQ == 0:
                    pe.wait_ge(vq_d, nth(QUADS, it, n // GPQ))
                    if not (first and n < 2 * GPQ):
                        pe.wait_ge(ob_d, nth(QUADS, it, n // GPQ - 2))
                    if n == GPQ and not first:
                        pe.wait_ge(x_d, it)
                for k, a in enumerate(heads):
                    for j in range(i + 1):
                        c = k * (i + 1) + j
                        ins = pe.matmul(bank[6 + quad % 2][:, (i * 4 + a) * HD:(i * 4 + a + 1) * HD], wT[:, n % 2, c * P:(c + 1) * P],
                                        vq[:, quad % 2, j, a * HD:(a + 1) * HD], start=j == 0, stop=j == i)
                ins.then_inc(av_d, 1)

            def max_dve(v, it, n, first):
                _, i, heads = GROUPS[n]
                m = 2 * len(heads)
                v.wait_ge(scored, nth(NG, it, n))
                lo = 2 * (n % 2)
                if i < 2:
                    half = m // 2
                    for h in range(2):
                        ins = v.tensor_reduce(negm[:, n % 2, h * half:(h + 1) * half],
                                              bank[lo + h][:].rearrange("p (m c) -> p m c", m=half), AX.X, ALU.max, negate=True)
                else:
                    for h in range(2):
                        ins = v.tensor_reduce(negm[:, n % 2, h:h + 1], bank[lo + h][:, 0:(i + 1) * P], AX.X, ALU.max, negate=True)
                ins.then_inc(maxed, 1)

            def exp_act(a_, it, n, first):
                quad, i, heads = GROUPS[n]
                a_.wait_ge(maxed, nth(NG, it, n))
                if not (first and n < 2):
                    a_.wait_ge(w_d, nth(NG, it, n - 2))
                if n % GPQ == 0 and not (first and n < 2 * GPQ):
                    a_.wait_ge(den_d, nth(QUADS, it, n // GPQ - 2))
                for k, a in enumerate(heads):
                    for st in range(2):
                        ins = a_.activation(ex_ap(n, i, k, st), s_ap(n, i, k, st), ACT.Exp,
                                            bias=negm[:, n % 2, 2 * k + st:2 * k + st + 1],
                                            accum_out=Z[:, quad % 2, i * 4 + a, st:st + 1])
                ins.then_inc(exped, 1)

            def combine_dve(v, it, n, first):
                quad, i, heads = GROUPS[n % NG]
                h, a, q, s = len(heads), heads[0], quad % 2, n % 2
                v.wait_ge(exped, nth(NG, it, n))
                z1, z2 = (Z[:, q, i * 4 + a:i * 4 + a + h, st] for st in range(2))
                v.reciprocal(rz2[:, s, 0:h], z2).then_inc(rz_d, 1)
                v.wait_ge(rz_d, nth(NG, it, n))
                v.tensor_tensor(ratio[:, s, 0:h], z1, rz2[:, s, 0:h], ALU.mult).then_inc(ratio_d, 1)
                v.wait_ge(ratio_d, nth(NG, it, n))
                v.tensor_tensor(coef[:, s, 0:h], ratio[:, s, 0:h], nlam[:, quad * 4 + a:quad * 4 + a + h], ALU.mult).then_inc(coef_d, 1)
                v.wait_ge(coef_d, nth(NG, it, n))
                if not (first and n < 2):
                    v.wait_ge(turned, nth(NG, it, n - 2))
                width = (i + 1) * P
                for k in range(h):
                    ins = v.scalar_tensor_tensor(out=w[:, s, k * width:(k + 1) * width], in0=ex_ap(n, i, k, 1),
                                                 scalar=coef[:, s, k:k + 1], in1=ex_ap(n, i, k, 0), op0=ALU.mult, op1=ALU.add)
                ins.then_inc(w_d, 1)
                v.wait_ge(w_d, nth(NG, it, n))
                v.tensor_reduce(asum[:, q, i * 4 + a:i * 4 + a + h], w[:, s, 0:h * width].rearrange("p (h c) -> p h c", h=h),
                                AX.X, ALU.add, apply_absolute_value=True).then_inc(asum_d, 1)

            def copy_wT_act(a_, it, n, first):
                _, i, heads = GROUPS[n % NG]
                a_.wait_ge(turned, nth(NG, it, n))
                if not (first and n < 2):
                    a_.wait_ge(av_d, nth(NG, it, n - 2))
                cols = len(heads) * (i + 1) * P
                a_.copy(wT[:, n % 2, 0:cols], bank[4 + n % 2][:, 0:cols]).then_inc(wT_d, 1)

            def finish_quad_dve(v, it, quad, first):
                q = quad % 2
                v.wait_ge(asum_d, nth(NG, it, (quad + 1) * GPQ - 1))
                v.scalar_tensor_tensor(out=den[:, q, :], in0=Z[:, q, :, 0], scalar=DENOM_MIN, in1=asum[:, q, :],
                                       op0=ALU.mult, op1=ALU.max).then_inc(den_d, 1)
                v.wait_ge(den_d, nth(QUADS, it, quad))
                v.reciprocal(rden[:, q, :], den[:, q, :]).then_inc(rden_d, 1)
                v.wait_ge(rden_d, nth(QUADS, it, quad))
                v.wait_ge(av_d, nth(NG, it, (quad + 1) * GPQ - 1))
                if quad == 0 and not first:
                    v.wait_ge(obT_p, it)
                qq = quad % QUADS
                v.tensor_tensor(ob[:, :, qq * 32:(qq + 1) * 32].rearrange("p i (a d) -> p i a d", a=4),
                                bank[6 + q][:, 0:16 * HD].rearrange("p (i a d) -> p i a d", i=4, a=4),
                                rden[:, q, :].rearrange("p (i a o) -> p i a o", i=4, o=1).to_broadcast([P, 4, 4, HD]),
                                ALU.mult).then_inc(ob_d, 1)

            OUT_STEP = 5

            def steps(eng, body, tail):
                body(eng, 0, True, False)
                with eng.Fori(1, BATCH) as it:
                    body(eng, it, False, False)
                body(eng, BATCH, False, True)

            def runs(n, first, tail):
                return (n >= 0 and not tail) or (n < 0 and not first)

            def body_pe(pe, it, first, tail):
                for n in range(10 if tail else NG):
                    if runs(n, first, tail):
                        scores_pe(pe, it, n, first)
                    if runs(n - 2, first, tail):
                        turn_pe(pe, it, n - 2, first)
                    if runs(n - 3, first, tail):
                        av_pe(pe, it, n - 3, first)
                    if n == OUT_STEP and not first:
                        pe.wait_ge(ob_d, nth(QUADS, it, -1))
                        for j in range(BPB):
                            ins = pe.transpose(bank[7][:, j * P:(j + 1) * P], ob[:, j, :], ident[:])
                        ins.then_inc(obT_p, 1)
                    if n == OUT_STEP + 2 and not first:
                        pe.wait_ge(obT_d, it)
                        for j in range(BPB):
                            ins = pe.matmul(bank[7][:, j * P:(j + 1) * P], obT[:, j * P:(j + 1) * P], WT[:, 4, :], start=True, stop=True)
                        ins.then_inc(op_p, 1)

            def body_act(a, it, first, tail):
                for n in range(10 if tail else NG):
                    if runs(n, first, tail):
                        exp_act(a, it, n, first)
                    if runs(n - 2, first, tail):
                        copy_wT_act(a, it, n - 2, first)
                    if n == OUT_STEP + 1 and not first:
                        a.wait_ge(obT_p, it)
                        a.copy(obT[:], bank[7][:]).then_inc(obT_d, 1)

            def body_dve(v, it, first, tail):
                for n in range(10 if tail else NG):
                    if runs(n, first, tail):
                        max_dve(v, it, n, first)
                    if runs(n - 1, first, tail):
                        combine_dve(v, it, n - 1, first)
                    if n % GPQ == 4 and runs(n - GPQ, first, tail):
                        finish_quad_dve(v, it, n // GPQ - 1, first)
                    if n == OUT_STEP + 3 and not first:
                        v.wait_ge(op_p, it)
                        xb = X[:, bass.ds((it - 1) * BPB, BPB), :]
                        v.tensor_tensor(xb, bank[7][:].rearrange("p (j d) -> p j d", d=D), xb, ALU.add).then_inc(x_d, 1)

            def body_sp(sp, it, quads=QUADS, first=False, tail=False):
                for quad in range(QUADS):
                    s = quad % 2
                    if not (first and quad < 2):
                        sp.wait_ge(scored, nth(NG, it, (quad - 1) * GPQ - 1))
                    for t in range(3):
                        for par in range(2):
                            sp.dma_start(stack[64 * par:64 * par + ROWS, s, t, :, :],
                                         KD[t, bass.ds(it, 1), quad * 2 + par, :, :].rearrange("b (r h) n -> (b r) h n", h=2)
                                         ).then_inc(loaded[s], 16)

            def body_pool(pool, it, first):
                for quad in range(QUADS):
                    if not (first and quad < 2):
                        pool.wait_ge(av_d, nth(NG, it, (quad - 1) * GPQ - 1))
                    pool.tensor_copy(vq[:, quad % 2], V[:, bass.ds(it * BPB, BPB), quad * 32:(quad + 1) * 32]).then_inc(vq_d, 1)

            def sp_part(sp):
                over_batches(sp, proj_sp)
                for s in range(2):
                    sp.wait_ge(kd_out[s], 2 * 3 * TERMS * 16)
                body_sp(sp, 0, first=True)
                with sp.Fori(1, BATCH) as it:
                    body_sp(sp, it)

            def pool_part(pool):
                over_batches(pool, norm.pool)
                pool.wait_ge(v_d, BATCH)
                body_pool(pool, 0, True)
                with pool.Fori(1, BATCH) as it:
                    body_pool(pool, it, False)

            def dve_part(v):
                v.wait_ge(x_ready, BATCH)
                over_batches(v, proj_dve)
                steps(v, body_dve, None)

            def act_part(a):
                over_batches(a, proj_act)
                steps(a, body_act, None)

            def pe_part(pe):
                over_batches(pe, proj_pe)
                pe.wait_ge(v_d, BATCH)
                pe.wait_ge(res1, 3 * BATCH)
                steps(pe, body_pe, None)

            return dict(sp=sp_part, pool=pool_part, dve=dve_part, act=act_part, pe=pe_part), x_d

        def x_loaded(v):
            v.wait_ge(x_in, 16)

        ffn1, x1 = ffn("f1", x_loaded, False)
        attn, x2 = attention(x1)

        def x_attended(v):
            v.wait_ge(x2, BATCH)

        ffn2, _ = ffn("f2", x_attended, True)

        block = ctx.enter_context(nc.Block())

        @block.sync
        def _(sp):
            setup_sp(sp)
            ffn1["sp"](sp)
            attn["sp"](sp)
            ffn2["sp"](sp)

        @block.gpsimd
        def _(pool):
            setup_pool(pool)
            ffn1["pool"](pool)
            attn["pool"](pool)
            ffn2["pool"](pool)

        @block.vector
        def _(v):
            setup_dve(v)
            ffn1["dve"](v)
            attn["dve"](v)
            ffn2["dve"](v)

        @block.scalar
        def _(a):
            setup_act(a)
            ffn1["act"](a)
            attn["act"](a)
            ffn2["act"](a)

        @block.tensor
        def _(pe):
            setup_pe(pe)
            pe.wait_ge(dve_set, DVE_SET)
            ffn1["pe"](pe)
            attn["pe"](pe)
            ffn2["pe"](pe)


_INS = ["L0_attn_x", "L0_attn_Wq", "L0_attn_Wk1", "L0_attn_Wk2", "L0_attn_Wv", "L0_attn_Wo", "L0_attn_lambda_logit",
        "L0_ffn_wr", "L0_ffn_br", "L0_ffn_w1", "L0_ffn_b1", "L0_ffn_w2", "L0_ffn_b2"]


def kernel(**inputs):
    import numpy as _np
    import concourse.bacc as _bacc
    from concourse import mybir as _mybir
    from concourse.bass_utils import run_bass_kernel_spmd as _run

    nc = _bacc.Bacc("TRN2", target_bir_lowering=False, num_devices=1)
    arrays, args = {}, []
    for name in _INS:
        a = _np.ascontiguousarray(inputs[name])
        arrays[f"in_{name}_dram"] = a
        args.append(nc.dram_tensor(f"in_{name}_dram", a.shape, _mybir.dt.from_np(a.dtype), kind="ExternalInput").ap())
    out = nc.dram_tensor("out_0_dram", (BATCH, SEQ, D), _mybir.dt.float32, kind="ExternalOutput").ap()
    build(nc, *args, out)
    r = _run(nc, [arrays], core_ids=[0])
    return r.results[0]["out_0_dram"]
```

```python
from contextlib import ExitStack

import concourse.bass as bass
from concourse import mybir

ALU = mybir.AluOpType
ACT = mybir.ActivationFunctionType
AX = mybir.AxisListType
F32 = mybir.dt.float32
BF16 = mybir.dt.bfloat16
I32 = mybir.dt.int32
U32 = mybir.dt.uint32

P = 128
BATCH, SEQ, D = 4, 512, 128
NBLK = BATCH * SEQ // P
BPB = SEQ // P
HEADS, HD = 16, 8
E, F = 8, 512
FC = F // P
LN_EPS = 1e-5
SCALE = HD ** -0.5
DENOM_MIN = 1e-6
MASKED = -3.0e38

REGION = BATCH * SEQ + P
TILES = NBLK + E - 1
SPARE = E * REGION

Q_PARTS = [0, 0, 0, 1, 1, 2]
K_PARTS = [0, 1, 2, 0, 1, 0]
TERMS = len(Q_PARTS)
ROWS = TERMS * HD
QUADS = HEADS // 4

GROUPS_OF_QUAD = ([(3, [a]) for a in range(4)] + [(2, [a]) for a in range(4)]
                  + [(1, [0, 1]), (1, [2, 3])] + [(0, [0, 1, 2, 3])])
GPQ = len(GROUPS_OF_QUAD)
GROUPS = [(quad, i, heads) for quad in range(QUADS) for i, heads in GROUPS_OF_QUAD]
NG = len(GROUPS)
ROUND_ENDS = [g for g in range(GPQ) if g == GPQ - 1 or GROUPS_OF_QUAD[g][0] != GROUPS_OF_QUAD[g + 1][0]]
ROUNDS = len(ROUND_ENDS) * QUADS
W_SLOTS = 4
EX_SLOTS = 4
W_LAG, ABS_LAG, TURN_LAG, AV_LAG = 2, 3, 4, 6
FINISH_STEP = 8


def nth(per, it, n):
    return it * per + (n + 1)


def build(nc, x, wq, wk1, wk2, wv, wo, lam, wr, br, w1, b1, w2, b2, out):
    with ExitStack() as ctx:
        def sb(name, shape, dt=F32):
            return ctx.enter_context(nc.sbuf_tensor(name, shape, dt))

        def sem(name):
            return ctx.enter_context(nc.semaphore(name))

        bank = [ctx.enter_context(nc.psum_tensor(f"bank{i}", [P, 512], F32)) for i in range(8)]

        X = sb("X", [P, NBLK, D])
        W1 = sb("W1", [P, E * F])
        W2 = sb("W2", [P, E * FC * D])
        WT = sb("WT", [P, 5, D])
        wraw = sb("wraw", [P, 5, D])
        wr_sb = sb("wr_sb", [P, E])
        br_sb = sb("br_sb", [1, E])
        B1S = sb("B1S", [3, E * F], BF16)
        B2S = sb("B2S", [3, E * D], BF16)
        ident = sb("ident", [P, P])
        identb = sb("identb", [P, P], BF16)
        maskb = sb("maskb", [P, P], BF16)
        trib = sb("trib", [P, P], BF16)
        onesb = sb("onesb", [P, P], BF16)
        ones1 = sb("ones1", [1, P])
        zeros = sb("zeros", [P, D])
        mhalf = sb("mhalf", [P, BPB])
        nlam = sb("nlam", [P, HEADS])
        lamt = sb("lamt", [P, 2, HEADS])
        em8 = sb("em8", [P, E])
        ereg = sb("ereg", [P, E])
        tri8 = sb("tri8", [P, E, E])
        iot = sb("iot", [P, TILES])
        iot128 = sb("iot128", [P, TILES])
        e9 = sb("e9", [P, E + 1])
        braw = sb("braw", [P, E * F // P + E * D // P])
        bres = sb("bres", [P, 2, E * F // P + E * D // P])
        bpart = sb("bpart", [P, 3, E * F // P + E * D // P], BF16)

        stats = sb("stats", [P, 2, BPB, 6])
        mv = sb("mv", [P, 2, BPB, 2])
        veps = sb("veps", [P, 2, BPB])
        rstd = sb("rstd", [P, 2, BPB])
        xn = sb("xn", [P, 2, BPB, D])
        xnT = sb("xnT", [P, 2, SEQ])
        rmax = sb("rmax", [P, 2, BPB])
        req = sb("req", [P, 2, BPB, E])
        rcand = sb("rcand", [P, 2, BPB, E])
        rmin = sb("rmin", [P, 2, BPB])
        OH = sb("OH", [P, NBLK, E], BF16)
        seen = sb("seen", [P, E], BF16)
        seenf = sb("seenf", [P, 2, E])
        place = sb("place", [P, 2, BPB, E])
        SLOT = sb("SLOT", [P, NBLK])
        slotu = sb("slotu", [P, 2, BPB], U32)
        cnt = sb("cnt", [P, E])
        cnti = sb("cnti", [P, E], I32)
        ntile = sb("ntile", [P, E])
        ntilei = sb("ntilei", [P, E], I32)
        cprod = sb("cprod", [P, E, E])
        cend = sb("cend", [P, E])
        cstart = sb("cstart", [P, E])
        shift = sb("shift", [P, E])
        tge = sb("tge", [P, TILES, E])
        texp = sb("texp", [P, TILES])
        tone = sb("tone", [P, TILES, E + 1])
        trow = sb("trow", [P, TILES, E + 1])
        trowf = sb("trowf", [P, TILES])
        tilee = sb("tilee", [P, TILES], I32)
        tiler = sb("tiler", [P, TILES], I32)
        yprod = sb("yprod", [P, NBLK, E])
        ysub = sb("ysub", [P, NBLK])
        yslot = sb("yslot", [P, NBLK], U32)
        YG = sb("YG", [P, NBLK, D])

        tin = sb("tin", [P, 2, D])
        tinT = sb("tinT", [P, 2, P])
        hid = sb("hid", [P, 2, F])
        hidT = sb("hidT", [P, 2, FC, P])
        ytile = sb("ytile", [P, 2, D])

        V = sb("V", [P, NBLK, D])
        parts = sb("parts", [P, 2, 3, 3, SEQ], BF16)
        resid = sb("resid", [P, 3, SEQ])
        stack = sb("stack", [P, 2, 3, 2, SEQ], BF16)
        negm = sb("negm", [P, 2, 2, 4])
        ex = sb("ex", [P, EX_SLOTS, 1024])
        w = sb("w", [P, W_SLOTS, 512])
        absw = sb("absw", [P, 512])
        wT = sb("wT", [P, 2, 4, 512])
        oT = sb("oT", [P, SEQ])
        Z = sb("Z", [P, 2, 16, 2])
        rz2 = sb("rz2", [P, 2, 4])
        ratio = sb("ratio", [P, 2, 4])
        coef = sb("coef", [P, 2, 4])
        asum = sb("asum", [P, 2, 16])
        den = sb("den", [P, 2, 16])
        rden = sb("rden", [P, 2, 16])
        vq = sb("vq", [P, 2, BPB, 32])
        ob = sb("ob", [P, BPB, D])
        obT = sb("obT", [P, SEQ])

        XS = nc.dram_tensor("rows_by_expert", [SPARE + P, D], F32, kind="Internal").ap()
        YS = nc.dram_tensor("rows_by_tile", [TILES * P, D], F32, kind="Internal").ap()
        KD = nc.dram_tensor("stacks", [3, BATCH, QUADS * 2, ROWS * 2, SEQ], BF16, kind="Internal").ap()

        x_in = sem("x_in")
        small_in = sem("small_in")
        w1_in = sem("w1_in")
        w2_in = sem("w2_in")
        pool_set = sem("pool_set")
        dve_set = sem("dve_set")
        act_set = sem("act_set")
        pe_set = sem("pe_set")
        bias_in = sem("bias_in")
        spare_zero = sem("spare_zero")
        out_stored = sem("out_stored")

        NSET_POOL = 17

        def setup_sp(sp):
            sp.dma_start(X[:], x.rearrange("b (t p) d -> p (b t) d", p=P)).then_inc(x_in, 16)
            for t, src in enumerate((wq, wk1, wk2, wv, wo)):
                sp.dma_start(wraw[:, t, :], src).then_inc(small_in, 16)
            sp.dma_start(wr_sb[:], wr).then_inc(small_in, 16)
            sp.dma_start(br_sb[:], br.rearrange("(a e) -> a e", a=1)).then_inc(small_in, 16)
            sp.dma_start(lamt[:, 0, :], lam.rearrange("(a e) -> a e", a=1).to_broadcast([P, HEADS])).then_inc(small_in, 16)
            sp.dma_start(braw[:, 0:E * F // P], b1.rearrange("e (a f) -> (e a) f", a=P // E)).then_inc(small_in, 16)
            sp.dma_start(braw[:, E * F // P:], b2.rearrange("e (a f) -> (e a) f", a=P // E)).then_inc(small_in, 16)
            sp.dma_start(W1[:].rearrange("p (e f) -> p e f", e=E), w1.rearrange("e h f -> h e f")).then_inc(w1_in, 16)
            sp.dma_start(W2[:].rearrange("p (e c h) -> p e c h", e=E, c=FC),
                         w2.rearrange("e (c p) h -> p e c h", p=P)).then_inc(w2_in, 16)
            sp.wait_ge(dve_set, 4 + 5)
            for k in range(3):
                sp.dma_start(B1S[k:k + 1, :], bpart[:, k, 0:E * F // P]).then_inc(bias_in, 16)
                sp.dma_start(B2S[k:k + 1, :], bpart[:, k, E * F // P:]).then_inc(bias_in, 16)
            sp.wait_ge(pool_set, NSET_POOL)
            sp.dma_start(XS[SPARE:SPARE + P, :], zeros[:]).then_inc(spare_zero, 16)

        def setup_pool(pool):
            n = [0]

            def step(ins):
                n[0] += 1
                return ins.then_inc(pool_set, 1)

            step(pool.memset(ident[:], 0.0))
            step(pool.memset(maskb[:], 0.0))
            step(pool.memset(onesb[:], 1.0))
            step(pool.memset(tri8[:], 1.0))
            step(pool.memset(zeros[:], 0.0))
            step(pool.memset(mhalf[:], -0.5))
            step(pool.memset(ones1[:], 1.0))
            step(pool.memset(seen[:], 0.0))
            pool.wait_ge(pool_set, n[0])
            step(pool.affine_select(out=ident[:], in_=ident[:], compare_op=ALU.not_equal, fill=1.0, base=0,
                                    pattern=[[-1, P]], channel_multiplier=1))
            step(pool.affine_select(out=maskb[:], in_=maskb[:], compare_op=ALU.is_ge, fill=MASKED, base=0,
                                    pattern=[[-1, P]], channel_multiplier=1))
            step(pool.affine_select(out=trib[:], in_=onesb[:], compare_op=ALU.is_gt, fill=0.0, base=0,
                                    pattern=[[1, P]], channel_multiplier=-1))
            step(pool.affine_select(out=tri8[:], in_=tri8[:], compare_op=ALU.is_ge, fill=0.0, base=0,
                                    pattern=[[1, E], [-1, E]], channel_multiplier=0))
            for t, base, k, m in ((em8, -8, 1, E), (ereg, 0, REGION, E), (e9, 0, 1, E + 1), (iot, 0, 1, TILES),
                                  (iot128, 0, P, TILES)):
                step(pool.iota(t[:], pattern=[[k, m]], base=base, channel_multiplier=0,
                               allow_small_or_imprecise_dtypes=True))
            assert n[0] == NSET_POOL

        def setup_dve(v):
            v.wait_ge(small_in, 16 * 10)
            v.tensor_copy(bpart[:, 0, :], braw[:]).then_inc(dve_set, 1)
            v.wait_ge(dve_set, 1)
            v.tensor_tensor(bres[:, 0, :], braw[:], bpart[:, 0, :], ALU.subtract).then_inc(dve_set, 1)
            v.wait_ge(dve_set, 2)
            v.tensor_copy(bpart[:, 1, :], bres[:, 0, :]).then_inc(dve_set, 1)
            v.wait_ge(dve_set, 3)
            v.tensor_tensor(bpart[:, 2, :], bres[:, 0, :], bpart[:, 1, :], ALU.subtract).then_inc(dve_set, 1)
            v.wait_ge(pool_set, NSET_POOL)
            v.tensor_copy(identb[:], ident[:]).then_inc(dve_set, 1)
            v.wait_ge(act_set, 1)
            v.tensor_scalar(lamt[:, 0, :], lamt[:, 1, :], 1.0, -1.0, ALU.add, ALU.mult).then_inc(dve_set, 1)
            v.wait_ge(dve_set, 6)
            v.reciprocal(nlam[:], lamt[:, 0, :]).then_inc(dve_set, 1)
            v.memset(trow[:, :, E:E + 1], float(SPARE)).then_inc(dve_set, 1)
            v.wait_ge(pe_set, 1)
            for t in range(3):
                v.tensor_copy(WT[:, t, :].rearrange("k (g d h) -> k g d h", h=2, d=HD),
                              bank[0][:, t * D:(t + 1) * D].rearrange("k (g h d) -> k g d h", h=2, d=HD)).then_inc(dve_set, 1)
            v.tensor_copy(WT[:, 3, :], bank[0][:, 3 * D:4 * D]).then_inc(dve_set, 1)
            v.tensor_copy(WT[:, 4, :], bank[1][:, 0:D]).then_inc(dve_set, 1)

        def setup_act(a):
            a.wait_ge(small_in, 16 * 10)
            a.activation(lamt[:, 1, :], lamt[:, 0, :], ACT.Exp, scale=-1.0).then_inc(act_set, 1)

        def setup_pe(pe):
            pe.wait_ge(small_in, 16 * 10)
            pe.wait_ge(pool_set, NSET_POOL)
            for t in range(5):
                last = pe.transpose(bank[t // 4][:, (t % 4) * D:(t % 4 + 1) * D], wraw[:, t, :], ident[:])
            last.then_inc(pe_set, 1)

        DVE_SET = 13

        class Norm:

            def __init__(self, tag):
                self.stat = sem(f"{tag}_stat")
                self.mv = sem(f"{tag}_mv")
                self.veps = sem(f"{tag}_veps")
                self.rstd = sem(f"{tag}_rstd")
                self.xn = sem(f"{tag}_xn")
                self.tr = sem(f"{tag}_tr")
                self.xnT = sem(f"{tag}_xnT")

            def dve_stats(self, v, b, s):
                for j in range(BPB):
                    v.bn_stats(stats[:, s, j, :], X[:, bass.ds(b * BPB + j, 1), :]).then_inc(self.stat, 1)
                v.wait_ge(self.stat, (b + 1) * BPB)
                for j in range(BPB):
                    ins = v.bn_aggr(mv[:, s, j, :], stats[:, s, j, :])
                ins.then_inc(self.mv, 1)

            def pool(self, pool, b, s):
                pool.wait_ge(self.mv, b + 1)
                pool.tensor_scalar(veps[:, s, :], mv[:, s, :, 1], LN_EPS, None, ALU.add).then_inc(self.veps, 1)
                pool.wait_ge(self.veps, b + 1)
                pool.tensor_tensor(rstd[:, s, :], veps[:, s, :], mhalf[:], ALU.pow).then_inc(self.rstd, 1)

            def dve_apply(self, v, b, s):
                v.wait_ge(self.rstd, b + 1)
                for j in range(BPB):
                    ins = v.tensor_scalar(xn[:, s, j, :], X[:, bass.ds(b * BPB + j, 1), :], mv[:, s, j, 0:1],
                                          rstd[:, s, j:j + 1], ALU.subtract, ALU.mult)
                ins.then_inc(self.xn, 1)

            def pe(self, pe, b, s):
                pe.wait_ge(self.xn, b + 1)
                for j in range(BPB):
                    ins = pe.transpose(bank[s][:, j * P:(j + 1) * P], xn[:, s, j, :], ident[:])
                ins.then_inc(self.tr, 1)

            def act(self, a, b, s):
                a.wait_ge(self.tr, b + 1)
                a.copy(xnT[:, s, :], bank[s][:]).then_inc(self.xnT, 1)

        def ffn(tag, before, store):
            norm = Norm(tag)
            score = sem(f"{tag}_score")
            rmax_d = sem(f"{tag}_rmax")
            req_d = sem(f"{tag}_req")
            cand_d = sem(f"{tag}_cand")
            rmin_d = sem(f"{tag}_rmin")
            oh_d = sem(f"{tag}_oh")
            rank = sem(f"{tag}_rank")
            sum_d = sem(f"{tag}_sum")
            seen_d = sem(f"{tag}_seen")
            place_d = sem(f"{tag}_place")
            slot_d = sem(f"{tag}_slot")
            scattered = [sem(f"{tag}_scattered{s}") for s in range(2)]
            count_p = sem(f"{tag}_count")
            table = sem(f"{tag}_table")
            padded = sem(f"{tag}_padded")
            tin_in = [sem(f"{tag}_tin{s}") for s in range(2)]
            tinT_p = sem(f"{tag}_tinT_p")
            tinT_d = sem(f"{tag}_tinT")
            hid_p = sem(f"{tag}_hid_p")
            hid_d = sem(f"{tag}_hid")
            hidT_p = sem(f"{tag}_hidT_p")
            hidT_d = sem(f"{tag}_hidT")
            y_p = sem(f"{tag}_y_p")
            y_d = sem(f"{tag}_y")
            y_out = [sem(f"{tag}_y_out{s}") for s in range(2)]
            gathered = [sem(f"{tag}_gathered{b}") for b in range(BATCH)]
            x_d = sem(f"{tag}_x")

            def route_dve(v, b, s):
                blocks = bass.ds(b * BPB, BPB)
                sc = bank[2 + s][:, 0:BPB * E].rearrange("p (j e) -> p j e", e=E)
                em8b = em8[:].rearrange("p (a e) -> p a e", a=1).to_broadcast([P, BPB, E])

                def over_e(t):
                    return t.rearrange("p (j a) -> p j a", a=1).to_broadcast([P, BPB, E])

                norm.dve_stats(v, b, s)
                if not (isinstance(b, int) and b < 2):
                    v.wait_ge(scattered[s], (b - s) * (8 * BPB))
                norm.dve_apply(v, b, s)
                v.wait_ge(score, b + 1)
                v.tensor_reduce(rmax[:, s, :], sc, AX.X, ALU.max).then_inc(rmax_d, 1)
                v.wait_ge(rmax_d, b + 1)
                v.tensor_tensor(req[:, s], sc, over_e(rmax[:, s, :]), ALU.is_equal).then_inc(req_d, 1)
                v.wait_ge(req_d, b + 1)
                v.tensor_tensor(rcand[:, s], req[:, s], em8b, ALU.mult).then_inc(cand_d, 1)
                v.wait_ge(cand_d, b + 1)
                v.tensor_reduce(rmin[:, s, :], rcand[:, s], AX.X, ALU.min).then_inc(rmin_d, 1)
                v.wait_ge(rmin_d, b + 1)
                v.tensor_tensor(OH[:, blocks, :], em8b, over_e(rmin[:, s, :]), ALU.is_equal).then_inc(oh_d, 1)
                v.wait_ge(oh_d, b + 1)
                v.tensor_reduce(seenf[:, s, :], OH[:, blocks, :].rearrange("p j e -> p e j"), AX.X, ALU.add).then_inc(sum_d, 1)
                v.wait_ge(rank, b + 1)
                v.tensor_tensor(place[:, s], bank[4 + s][:, 0:BPB * E].rearrange("p (j e) -> p j e", e=E),
                                ereg[:].rearrange("p (a e) -> p a e", a=1).to_broadcast([P, BPB, E]), ALU.add).then_inc(place_d, 1)
                v.wait_ge(sum_d, b + 1)
                v.tensor_tensor(seen[:], seen[:], seenf[:, s, :], ALU.add).then_inc(seen_d, 1)
                v.wait_ge(place_d, 2 * b + 1)
                v.tensor_tensor(place[:, s], place[:, s], OH[:, blocks, :], ALU.mult).then_inc(place_d, 1)
                v.wait_ge(place_d, 2 * b + 2)
                v.tensor_reduce(SLOT[:, blocks], place[:, s], AX.X, ALU.add).then_inc(slot_d, 1)
                v.wait_ge(slot_d, 2 * b + 1)
                v.tensor_copy(slotu[:, s, :], SLOT[:, blocks]).then_inc(slot_d, 1)

            def route_pe(pe, b, s):
                norm.pe(pe, b, s)
                pe.wait_ge(norm.xnT, b + 1)
                for j in range(BPB):
                    o = bank[2 + s][:, j * E:(j + 1) * E]
                    pe.matmul(o, ones1[:], br_sb[:], start=True, stop=False)
                    ins = pe.matmul(o, xnT[:, s, j * P:(j + 1) * P], wr_sb[:], start=False, stop=True)
                ins.then_inc(score, 1)
                pe.wait_ge(oh_d, b + 1)
                if not (isinstance(b, int) and b == 0):
                    pe.wait_ge(seen_d, b)
                r = bank[4 + s][:, 0:BPB * E].rearrange("p (j e) -> p j e", e=E)
                pe.matmul(r, onesb[:], seen[:].rearrange("p (a e) -> p a e", a=1).to_broadcast([P, BPB, E]),
                          start=True, stop=False, skip_group_check=True)
                for j in range(BPB - 1):
                    pe.matmul(r[:, j + 1:, :], onesb[:], OH[:, bass.ds(b * BPB + j, 1), :].to_broadcast([P, BPB - 1 - j, E]),
                              start=False, stop=False, skip_group_check=True)
                for j in range(BPB):
                    ins = pe.matmul(r[:, j, :], trib[:], OH[:, bass.ds(b * BPB + j, 1), :],
                                    start=False, stop=j == BPB - 1, skip_group_check=True)
                ins.then_inc(rank, 1)

            def route_pool(pool, b, s):
                norm.pool(pool, b, s)
                pool.wait_ge(slot_d, 2 * b + 2)
                for j in range(BPB):
                    pool.indirect_dma_start(out=XS, out_offset=bass.IndirectOffsetOnAxis(ap=slotu[:, s, j:j + 1], axis=0),
                                            in_=xn[:, s, j, :], in_offset=None).then_inc(scattered[s], 16)

            def over_batches(eng, body):
                for b in range(2):
                    body(eng, b, b)
                with eng.Fori(1, BATCH // 2) as pair:
                    for s in range(2):
                        body(eng, pair * 2 + s, s)

            def table_dve(v):
                n = [0]

                def step(ins):
                    ins.then_inc(table, 1)
                    n[0] += 1
                    v.wait_ge(table, n[0])

                def mid(t, k, m):
                    return t.rearrange("p (a e) -> p a e", a=1).to_broadcast([P, k, m])

                def last(t, k, m):
                    return t.rearrange("p (j a) -> p j a", a=1).to_broadcast([P, k, m])

                v.wait_ge(count_p, 1)
                step(v.tensor_copy(cnt[:], bank[6][:, 0:E]))
                step(v.tensor_copy(cnti[:], cnt[:]))
                step(v.tensor_scalar(ntile[:], cnt[:], 1.0 / P, (P - 1) / (2.0 * P), ALU.mult, ALU.add))
                step(v.tensor_copy(ntilei[:], ntile[:]))
                step(v.tensor_copy(ntile[:], ntilei[:]))
                step(v.tensor_tensor(cprod[:], tri8[:], mid(ntile[:], E, E), ALU.mult))
                step(v.tensor_reduce(cend[:], cprod[:], AX.X, ALU.add))
                step(v.tensor_tensor(cstart[:], cend[:], ntile[:], ALU.subtract))
                step(v.scalar_tensor_tensor(out=shift[:], in0=cstart[:], scalar=-float(P), in1=ereg[:],
                                            op0=ALU.mult, op1=ALU.add))
                step(v.tensor_tensor(tge[:], last(iot[:], TILES, E), mid(cend[:], TILES, E), ALU.is_ge))
                step(v.tensor_reduce(texp[:], tge[:], AX.X, ALU.add))
                step(v.tensor_tensor(tone[:], last(texp[:], TILES, E + 1), mid(e9[:], TILES, E + 1), ALU.is_equal))
                step(v.tensor_tensor(trow[:, :, 0:E], last(iot128[:], TILES, E), mid(shift[:], TILES, E), ALU.add))
                step(v.tensor_tensor(tone[:], tone[:], trow[:], ALU.mult))
                step(v.tensor_reduce(trowf[:], tone[:], AX.X, ALU.add))
                step(v.tensor_copy(tiler[:], trowf[:]))
                step(v.tensor_scalar(tilee[:], texp[:], float(E - 1), None, ALU.min))
                step(v.tensor_tensor(yprod[:], OH[:], mid(shift[:], NBLK, E), ALU.mult))
                step(v.tensor_reduce(ysub[:], yprod[:], AX.X, ALU.add))
                step(v.tensor_tensor(yslot[:], SLOT[:], ysub[:], ALU.subtract))
                step(v.memset(seen[:], 0.0))
                assert n[0] == TABLE

            TABLE, TABLE_COUNTS, TABLE_TILES = 21, 2, 17

            def load_tile(sp, t, s):
                if not (isinstance(t, int) and t < 2):
                    sp.wait_ge(tinT_p, t - 1)
                row = sp.value_load(tiler[0:1, bass.ds(t, 1)], min_val=0, max_val=SPARE)
                sp.dma_start(tin[:, s, :], XS[bass.ds(row, P), :]).then_inc(tin_in[s], 16)

            def turn_in(pe, t, s):
                pe.wait_ge(tin_in[s], (t // 2 + 1) * 16 if isinstance(t, int) else (t - s) * 8 + 16)
                if not (isinstance(t, int) and t < 2):
                    pe.wait_ge(tinT_d, t - 1)
                pe.transpose(bank[s][:, 0:P], tin[:, s, :], ident[:]).then_inc(tinT_p, 1)

            def up(pe, t, s):
                e = pe.value_load(tilee[0:1, bass.ds(t, 1)], min_val=0, max_val=E - 1)
                pe.wait_ge(tinT_d, t + 1)
                if not (isinstance(t, int) and t < 2):
                    pe.wait_ge(hid_d, t - 1)
                pe.matmul(bank[2 + s][:], onesb[0:3, :], B1S[:, bass.ds(e * F, F)], start=True, stop=False)
                pe.matmul(bank[2 + s][:], tinT[:, s, :], W1[:, bass.ds(e * F, F)],
                          start=False, stop=True).then_inc(hid_p, 1)

            def turn_hidden(pe, t, s):
                pe.wait_ge(hid_d, t + 1)
                if not (isinstance(t, int) and t < 2):
                    pe.wait_ge(hidT_d, t - 1)
                for c in range(FC):
                    ins = pe.transpose(bank[4 + s][:, c * P:(c + 1) * P], hid[:, s, c * P:(c + 1) * P], ident[:])
                ins.then_inc(hidT_p, 1)

            def down(pe, t, s):
                e = pe.value_load(tilee[0:1, bass.ds(t, 1)], min_val=0, max_val=E - 1)
                pe.wait_ge(hidT_d, t + 1)
                if not (isinstance(t, int) and t < 2):
                    pe.wait_ge(y_d, t - 1)
                pe.matmul(bank[6 + s][:, 0:D], onesb[0:3, :], B2S[:, bass.ds(e * D, D)], start=True, stop=False)
                for c in range(FC):
                    ins = pe.matmul(bank[6 + s][:, 0:D], hidT[:, s, c, :], W2[:, bass.ds(e * (FC * D) + c * D, D)],
                                    start=False, stop=c == FC - 1)
                ins.then_inc(y_p, 1)

            def over_tiles(eng, step):
                for t in range(4):
                    step(eng, t, t % 2)
                with eng.Fori(2, (TILES - 1) // 2) as pair:
                    for s in range(2):
                        step(eng, pair * 2 + s, s)
                for t in range(TILES - 1, TILES + 2):
                    step(eng, t, t % 2)

            def known(t, lo, hi):
                return not isinstance(t, int) or lo <= t < hi

            def tile_pe(pe, t, s):
                if known(t, 0, TILES):
                    up(pe, t, s)
                if known(t, 1, TILES + 1):
                    turn_hidden(pe, t - 1, 1 - s)
                if known(t, 0, TILES - 1):
                    turn_in(pe, t + 1, 1 - s)
                if known(t, 2, TILES + 2):
                    down(pe, t - 2, s)

            def tile_act(a, t, s):
                if known(t, 0, TILES):
                    a.wait_ge(hid_p, t + 1)
                    if not (isinstance(t, int) and t < 2):
                        a.wait_ge(hidT_p, t - 1)
                    a.activation(hid[:, s, :], bank[2 + s][:], ACT.Gelu).then_inc(hid_d, 1)
                if known(t, 2, TILES + 2):
                    a.wait_ge(y_p, t - 1)
                    if not (isinstance(t, int) and t < 4):
                        a.wait_ge(y_out[s], (t // 2 - 1) * 16 if isinstance(t, int) else (t - s) * 8 - 16)
                    a.copy(ytile[:, s, :], bank[6 + s][:, 0:D]).then_inc(y_d, 1)
                    a.wait_ge(y_d, t - 1)
                    a.dma_start(YS[bass.ds((t - 2) * P, P), :], ytile[:, s, :]).then_inc(y_out[s], 16)

            def tile_dve(v, t, s):
                if known(t, 1, TILES + 1):
                    v.wait_ge(hidT_p, t)
                    if not (isinstance(t, int) and t < 3):
                        v.wait_ge(y_p, t - 2)
                    v.tensor_copy(hidT[:, 1 - s].rearrange("p c k -> p (c k)"), bank[4 + 1 - s][:]).then_inc(hidT_d, 1)
                if known(t, 0, TILES - 1):
                    v.wait_ge(tinT_p, t + 2)
                    if not (isinstance(t, int) and t < 1):
                        v.wait_ge(hid_p, t)
                    v.tensor_copy(tinT[:, 1 - s, :], bank[1 - s][:, 0:P]).then_inc(tinT_d, 1)

            def sp_part(sp):
                sp.wait_ge(table, TABLE_COUNTS)
                for e in range(E):
                    n = sp.value_load(cnti[0:1, e:e + 1], min_val=0, max_val=BATCH * SEQ)
                    sp.dma_start(XS[bass.ds(n + e * REGION, P), :], zeros[:]).then_inc(padded, 16)
                sp.wait_ge(table, TABLE_TILES)
                sp.wait_ge(padded, 16 * E)
                sp.wait_ge(spare_zero, 16)
                for s in range(2):
                    sp.wait_ge(scattered[s], 16 * NBLK // 2)
                for t in range(2):
                    load_tile(sp, t, t)
                with sp.Fori(1, (TILES - 1) // 2) as pair:
                    for s in range(2):
                        load_tile(sp, pair * 2 + s, s)
                load_tile(sp, TILES - 1, (TILES - 1) % 2)
                if store:
                    for b in range(BATCH):
                        sp.wait_ge(x_d, b + 1)
                        sp.dma_start(out[b].rearrange("(t p) d -> p t d", p=P), X[:, b * BPB:(b + 1) * BPB, :]).then_inc(out_stored, 16)
                    sp.wait_ge(out_stored, 16 * BATCH)

            def pool_part(pool):
                over_batches(pool, route_pool)
                pool.wait_ge(table, TABLE)
                for s in range(2):
                    pool.wait_ge(y_out[s], 16 * ((TILES + 1 - s) // 2))
                for t in range(NBLK):
                    pool.indirect_dma_start(out=YG[:, t, :], out_offset=None, in_=YS,
                                            in_offset=bass.IndirectOffsetOnAxis(ap=yslot[:, t:t + 1], axis=0)).then_inc(gathered[t // BPB], 16)

            def dve_part(v):
                before(v)
                over_batches(v, route_dve)
                table_dve(v)
                v.wait_ge(tinT_p, 1)
                v.tensor_copy(tinT[:, 0, :], bank[0][:, 0:P]).then_inc(tinT_d, 1)
                over_tiles(v, tile_dve)
                for b in range(BATCH):
                    v.wait_ge(gathered[b], 16 * BPB)
                    xb = X[:, b * BPB:(b + 1) * BPB, :]
                    v.scalar_tensor_tensor(out=xb, in0=YG[:, b * BPB:(b + 1) * BPB, :], scalar=0.5, in1=xb,
                                           op0=ALU.mult, op1=ALU.add).then_inc(x_d, 1)

            def act_part(a):
                over_batches(a, norm.act)
                over_tiles(a, tile_act)

            def pe_part(pe):
                over_batches(pe, route_pe)
                pe.wait_ge(seen_d, BATCH)
                pe.matmul(bank[6][:, 0:E], onesb[:], seen[:], start=True, stop=True).then_inc(count_p, 1)
                pe.wait_ge(table, TABLE_TILES)
                pe.wait_ge(w1_in, 16)
                pe.wait_ge(w2_in, 16)
                pe.wait_ge(bias_in, 16 * 6)
                turn_in(pe, 0, 0)
                over_tiles(pe, tile_pe)

            return dict(sp=sp_part, pool=pool_part, dve=dve_part, act=act_part, pe=pe_part), x_d

        def attention(x_ready):
            norm = Norm("at")
            proj = sem("at_proj")
            vproj = sem("at_vproj")
            high = sem("at_high")
            res1 = sem("at_res1")
            middle = sem("at_middle")
            low = sem("at_low")
            v_d = sem("at_v")
            kd_out = [sem(f"at_kd_out{s}") for s in range(2)]
            loaded = [sem(f"at_loaded{s}") for s in range(2)]
            scored = sem("at_scored")
            maxed = sem("at_maxed")
            exped = sem("at_exped")
            rz_d = sem("at_rz")
            ratio_d = sem("at_ratio")
            coef_d = sem("at_coef")
            w_d = sem("at_w")
            asum_d = sem("at_asum")
            turned = sem("at_turned")
            wT_d = sem("at_wT")
            av_d = sem("at_av")
            vq_d = sem("at_vq")
            asum_a = sem("at_asum_a")
            oT_d = sem("at_oT")
            back = sem("at_back")
            den_d = sem("at_den")
            rden_d = sem("at_rden")
            ob_d = sem("at_ob")
            obT_p = sem("at_obT_p")
            obT_d = sem("at_obT")
            op_p = sem("at_op_p")
            x_d = sem("at_x")

            def over_batches(eng, body):
                for b in range(2):
                    body(eng, b, b)
                with eng.Fori(1, BATCH // 2) as pair:
                    for s in range(2):
                        body(eng, pair * 2 + s, s)

            def late(b, k):
                return not (isinstance(b, int) and b < k)

            scales = (SCALE, 1.0, 1.0)

            def proj_dve(v, b, s):
                norm.dve_stats(v, b, s)
                if late(b, 2):
                    v.wait_ge(norm.tr, b - 1)
                norm.dve_apply(v, b, s)
                for t in range(3):
                    v.wait_ge(high, 3 * b + (t + 1))
                    if late(b, 1):
                        v.wait_ge(middle, 3 * b + (t - 2))
                    v.scalar_tensor_tensor(out=resid[:, t, :], in0=bank[2 + t][:], scalar=scales[t], in1=parts[:, s, t, 0, :],
                                           op0=ALU.mult, op1=ALU.subtract).then_inc(res1, 1)
                for t in range(3):
                    v.wait_ge(middle, 3 * b + (t + 1))
                    v.tensor_tensor(parts[:, s, t, 2, :], resid[:, t, :], parts[:, s, t, 1, :], ALU.subtract).then_inc(low, 1)

            def proj_pe(pe, b, s):
                norm.pe(pe, b, s)
                pe.wait_ge(norm.xnT, b + 1)
                for t in range(3):
                    if late(b, 1):
                        pe.wait_ge(res1, 3 * b + (t - 2))
                    pe.matmul(bank[2 + t][:], WT[:, t, :], xnT[:, s, :], start=True, stop=True).then_inc(proj, 1)
                if late(b, 1):
                    pe.wait_ge(v_d, b)
                for j in range(BPB):
                    ins = pe.matmul(bank[5][:, j * P:(j + 1) * P], xnT[:, s, j * P:(j + 1) * P], WT[:, 3, :], start=True, stop=True)
                ins.then_inc(vproj, 1)

            def proj_act(a, b, s):
                norm.act(a, b, s)
                if late(b, 2):
                    a.wait_ge(kd_out[s], (b - s) * (8 * 3 * TERMS))
                for t in range(3):
                    a.wait_ge(proj, 3 * b + (t + 1))
                    a.mul(parts[:, s, t, 0, :], bank[2 + t][:], scales[t]).then_inc(high, 1)
                a.wait_ge(vproj, b + 1)
                a.copy(V[:, bass.ds(b * BPB, BPB), :], bank[5][:].rearrange("p (j d) -> p j d", d=D)).then_inc(v_d, 1)
                for t in range(3):
                    a.wait_ge(res1, 3 * b + (t + 1))
                    a.copy(parts[:, s, t, 1, :], resid[:, t, :]).then_inc(middle, 1)

            def proj_sp(sp, b, s):
                sp.wait_ge(low, 3 * b + 3)
                for t in range(3):
                    for term, part in enumerate(Q_PARTS if t == 0 else K_PARTS):
                        sp.dma_start(KD[t, bass.ds(b, 1), :, term * 2 * HD:(term + 1) * 2 * HD, :],
                                     parts[:, s, t, part, :]).then_inc(kd_out[s], 16)

            def spot(i, k, st):
                return (2 * k + st) * (i + 1) * P if i < 2 else st * 512

            def s_ap(n, i, k, st, lo=0, hi=None):
                width = (i + 1) * P
                at = spot(i, k, st)
                b = bank[2 * (n % 2) + at // 512]
                return b[:, at % 512 + lo:at % 512 + (width if hi is None else hi)]

            def ex_ap(n, i, k, st):
                return ex[:, n % EX_SLOTS, spot(i, k, st):spot(i, k, st) + (i + 1) * P]

            def bank_items(n, h):
                _, i, heads = GROUPS[n]
                return [(k, st) for k in range(len(heads)) for st in range(2) if spot(i, k, st) // 512 == h]

            def half(n, h):
                return 2 * n + h

            def round_of(n):
                return n // GPQ * len(ROUND_ENDS) + (3 - GROUPS[n % NG][1])

            def starts_round(n):
                return n % GPQ == 0 or (n % GPQ - 1) in ROUND_ENDS

            def abs_on_act(n):
                return GROUPS[n % NG][1] == BPB - 1

            ACT_SUMS = sum(abs_on_act(n) for n in range(GPQ))
            DVE_SUMS = GPQ - ACT_SUMS

            def scores_pe(pe, it, n, first):
                quad, i, heads = GROUPS[n]
                slot = quad % 2
                if n % GPQ == 0:
                    pe.wait_ge(loaded[slot], (it * 2 + quad // 2 + 1) * (6 * 16))
                per_bank = (2 if i == 1 else 4) if i < 2 else 1
                for h in range(2):
                    if not (first and n < 2):
                        pe.wait_ge(exped, nth(2 * NG, it, half(n - 2, h)))
                    o = bank[2 * (n % 2) + h][:, 0:per_bank * (i + 1) * P].rearrange("p (m c) -> p m c", m=per_bank)[:, :, i * P:]
                    pe.matmul(o, identb[:], maskb[:].rearrange("p (a c) -> p a c", a=1).to_broadcast([P, per_bank, P]),
                              start=True, stop=False, skip_group_check=True)
                    for k, st in bank_items(n, h):
                        a = heads[k]
                        r = slice(64 * (a // 2), 64 * (a // 2) + ROWS)
                        ins = pe.matmul(s_ap(n, i, k, st), stack[r, slot, 0, a % 2, i * P:(i + 1) * P],
                                        stack[r, slot, 1 + st, a % 2, 0:(i + 1) * P],
                                        start=False, stop=True, skip_group_check=True)
                    ins.then_inc(scored, 1)

            def turn_pe(pe, it, n, first):
                _, i, heads = GROUPS[n % NG]
                pe.wait_ge(w_d, nth(NG, it, n))
                if not (first and n < 2):
                    pe.wait_ge(wT_d, nth(NG, it, n - 2))
                for c in range(len(heads) * (i + 1)):
                    ins = pe.transpose(bank[4 + n % 2][:, c * P:(c + 1) * P], w[:, n % W_SLOTS, c * P:(c + 1) * P], ident[:])
                ins.then_inc(turned, 1)

            def av_pe(pe, it, n, first):
                quad, i, _ = GROUPS[n % NG]
                pe.wait_ge(wT_d, nth(NG, it, n))
                if n % GPQ == ROUND_ENDS[0]:
                    pe.wait_ge(vq_d, nth(QUADS, it, n // GPQ))
                    if not (first and n < GPQ):
                        pe.wait_ge(oT_d, nth(QUADS, it, n // GPQ - 1))
                for j in range(i + 1):
                    for a in range(4):
                        ins = pe.matmul(bank[6][32 * a:32 * (a + 1), i * P:(i + 1) * P], vq[:, quad % 2, j, :],
                                        wT[:, round_of(n) % 2, a, j * P:(j + 1) * P],
                                        start=j == 0, stop=j == i, skip_group_check=True)
                ins.then_inc(av_d, 1)

            def back_pe(pe, it, quad, first):
                pe.wait_ge(oT_d, nth(QUADS, it, quad))
                if not (first and quad == 0):
                    pe.wait_ge(ob_d, nth(QUADS, it, quad - 1))
                if quad == 0 and not first:
                    pe.wait_ge(x_d, it)
                for i in range(BPB):
                    ins = pe.transpose(bank[7][:, i * P:(i + 1) * P], oT[:, i * P:(i + 1) * P], ident[:])
                ins.then_inc(back, 1)

            def max_dve(v, it, n, h):
                _, i, heads = GROUPS[n]
                m = len(bank_items(n, h))
                v.wait_ge(scored, nth(2 * NG, it, half(n, h)))
                v.tensor_reduce(negm[:, n % 2, h, 0:m],
                                bank[2 * (n % 2) + h][:, 0:m * (i + 1) * P].rearrange("p (m c) -> p m c", m=m),
                                AX.X, ALU.max, negate=True).then_inc(maxed, 1)

            def exp_act(a_, it, n, h, first):
                quad, i, heads = GROUPS[n]
                a_.wait_ge(maxed, nth(2 * NG, it, half(n, h)))
                if h == 0:
                    if not (first and n < EX_SLOTS):
                        a_.wait_ge(w_d, nth(NG, it, n - EX_SLOTS))
                    if n % GPQ == 0 and not (first and n < 2 * GPQ):
                        a_.wait_ge(den_d, nth(QUADS, it, n // GPQ - 2))
                for m, (k, st) in enumerate(bank_items(n, h)):
                    ins = a_.activation(ex_ap(n, i, k, st), s_ap(n, i, k, st), ACT.Exp,
                                        bias=negm[:, n % 2, h, m:m + 1],
                                        accum_out=Z[:, quad % 2, i * 4 + heads[k], st:st + 1])
                ins.then_inc(exped, 1)

            def of_heads(t, n, *more):
                quad, i, heads = GROUPS[n % NG]
                return t[(slice(None), quad % 2, slice(i * 4 + heads[0], i * 4 + heads[0] + len(heads))) + more]

            def recip_dve(v, it, n):
                v.wait_ge(exped, nth(2 * NG, it, half(n, 1)))
                v.reciprocal(rz2[:, n % 2, 0:len(GROUPS[n % NG][2])], of_heads(Z, n, 1)).then_inc(rz_d, 1)

            def coef_dve(v, it, n):
                quad, i, heads = GROUPS[n % NG]
                h, s = len(heads), n % 2
                lam_h = nlam[:, quad * 4 + heads[0]:quad * 4 + heads[0] + h]
                v.wait_ge(rz_d, nth(NG, it, n))
                if h == 1:
                    v.scalar_tensor_tensor(out=coef[:, s, 0:1], in0=of_heads(Z, n, 0), scalar=rz2[:, s, 0:1], in1=lam_h,
                                           op0=ALU.mult, op1=ALU.mult).then_inc(coef_d, 1)
                else:
                    v.tensor_tensor(ratio[:, s, 0:h], of_heads(Z, n, 0), rz2[:, s, 0:h], ALU.mult).then_inc(ratio_d, 1)
                    v.wait_ge(ratio_d, nth(3 * QUADS, it, n // GPQ * 3 + (n % GPQ - 8)))
                    v.tensor_tensor(coef[:, s, 0:h], ratio[:, s, 0:h], lam_h, ALU.mult).then_inc(coef_d, 1)

            def sum_index(n):
                same = [g for g in range(GPQ) if abs_on_act(g) == abs_on_act(n)]
                return n // GPQ * len(same) + same.index(n % GPQ)

            def w_dve(v, it, n, first):
                quad, i, heads = GROUPS[n % NG]
                v.wait_ge(coef_d, nth(NG, it, n))
                if not (first and n < W_SLOTS):
                    v.wait_ge(turned, nth(NG, it, n - W_SLOTS))
                    if abs_on_act(n - W_SLOTS):
                        v.wait_ge(asum_a, nth(ACT_SUMS * QUADS, it, sum_index(n - W_SLOTS)))
                width = (i + 1) * P
                for k in range(len(heads)):
                    ins = v.scalar_tensor_tensor(out=w[:, n % W_SLOTS, k * width:(k + 1) * width], in0=ex_ap(n, i, k, 1),
                                                 scalar=coef[:, n % 2, k:k + 1], in1=ex_ap(n, i, k, 0), op0=ALU.mult, op1=ALU.add)
                ins.then_inc(w_d, 1)

            def abs_dve(v, it, n):
                _, i, heads = GROUPS[n % NG]
                v.wait_ge(w_d, nth(NG, it, n))
                v.tensor_reduce(of_heads(asum, n), w[:, n % W_SLOTS, 0:len(heads) * (i + 1) * P].rearrange("p (h c) -> p h c", h=len(heads)),
                                AX.X, ALU.add, apply_absolute_value=True).then_inc(asum_d, 1)

            def abs_act(a_, it, n, first):
                _, i, heads = GROUPS[n % NG]
                cols = (i + 1) * P
                a_.wait_ge(w_d, nth(NG, it, n))
                if not (first and sum_index(n) == 0):
                    a_.wait_ge(asum_a, nth(ACT_SUMS * QUADS, it, sum_index(n) - 1))
                a_.activation(absw[:, 0:cols], w[:, n % W_SLOTS, 0:cols], ACT.Abs, accum_out=of_heads(asum, n)).then_inc(asum_a, 1)

            def copy_wT_act(a_, it, n, first):
                _, i, heads = GROUPS[n % NG]
                h, cols = len(heads), (i + 1) * P
                a_.wait_ge(turned, nth(NG, it, n))
                if starts_round(n) and not (first and round_of(n) < 2):
                    a_.wait_ge(av_d, nth(ROUNDS, it, round_of(n) - 2))
                a_.copy(wT[:, round_of(n) % 2, heads[0]:heads[0] + h, 0:cols],
                        bank[4 + n % 2][:, 0:h * cols].rearrange("p (h c) -> p h c", h=h)).then_inc(wT_d, 1)

            def copy_oT_act(a_, it, quad, first):
                a_.wait_ge(av_d, nth(ROUNDS, it, (quad + 1) * len(ROUND_ENDS) - 1))
                if not (first and quad == 0):
                    a_.wait_ge(back, nth(QUADS, it, quad - 1))
                a_.copy(oT[:], bank[6][:]).then_inc(oT_d, 1)

            def finish_quad_dve(v, it, quad, first):
                q = quad % 2
                v.wait_ge(asum_d, nth(DVE_SUMS * QUADS, it, (quad + 1) * DVE_SUMS - 1))
                v.wait_ge(asum_a, nth(ACT_SUMS * QUADS, it, (quad + 1) * ACT_SUMS - 1))
                v.scalar_tensor_tensor(out=den[:, q, :], in0=Z[:, q, :, 0], scalar=DENOM_MIN, in1=asum[:, q, :],
                                       op0=ALU.mult, op1=ALU.max).then_inc(den_d, 1)
                v.wait_ge(den_d, nth(QUADS, it, quad))
                v.reciprocal(rden[:, q, :], den[:, q, :]).then_inc(rden_d, 1)
                v.wait_ge(rden_d, nth(QUADS, it, quad))
                v.wait_ge(back, nth(QUADS, it, quad))
                if quad == 0 and not first:
                    v.wait_ge(obT_p, it)
                qq = quad % QUADS
                for a in range(4):
                    ins = v.tensor_tensor(ob[:, :, (qq * 4 + a) * HD:(qq * 4 + a + 1) * HD],
                                          bank[7][:].rearrange("p (i c) -> p i c", c=P)[:, :, 40 * a:40 * a + HD],
                                          rden[:, q, :].rearrange("p (i a o) -> p i a o", i=4, o=1)[:, :, a].to_broadcast([P, BPB, HD]),
                                          ALU.mult)
                ins.then_inc(ob_d, 1)

            OUT_STEP = FINISH_STEP + 1
            TAIL = OUT_STEP + 4

            def steps(eng, body):
                body(eng, 0, True, False)
                with eng.Fori(1, BATCH) as it:
                    body(eng, it, False, False)
                body(eng, BATCH, False, True)

            def runs(n, first, tail):
                return (n >= 0 and not tail) or (n < 0 and not first)

            def quad_done(n, after, first, tail):
                return n % GPQ == after and runs(n - after - 1, first, tail)

            def body_pe(pe, it, first, tail):
                for n in range(TAIL if tail else NG):
                    if runs(n, first, tail):
                        scores_pe(pe, it, n, first)
                    if runs(n - TURN_LAG, first, tail):
                        turn_pe(pe, it, n - TURN_LAG, first)
                    if (n - AV_LAG) % GPQ in ROUND_ENDS and runs(n - AV_LAG, first, tail):
                        av_pe(pe, it, n - AV_LAG, first)
                    if quad_done(n, FINISH_STEP - 1, first, tail):
                        back_pe(pe, it, n // GPQ - 1, first)
                    if n == OUT_STEP and not first:
                        pe.wait_ge(ob_d, nth(QUADS, it, -1))
                        for j in range(BPB):
                            ins = pe.transpose(bank[7][:, j * P:(j + 1) * P], ob[:, j, :], ident[:])
                        ins.then_inc(obT_p, 1)
                    if n == OUT_STEP + 2 and not first:
                        pe.wait_ge(obT_d, it)
                        for j in range(BPB):
                            ins = pe.matmul(bank[7][:, j * P:(j + 1) * P], obT[:, j * P:(j + 1) * P], WT[:, 4, :], start=True, stop=True)
                        ins.then_inc(op_p, 1)

            def body_act(a, it, first, tail):
                for n in range(TAIL if tail else NG):
                    if runs(n, first, tail):
                        exp_act(a, it, n, 0, first)
                    if runs(n - TURN_LAG, first, tail):
                        copy_wT_act(a, it, n - TURN_LAG, first)
                    if abs_on_act(n - ABS_LAG) and runs(n - ABS_LAG, first, tail):
                        abs_act(a, it, n - ABS_LAG, first)
                    if runs(n, first, tail):
                        exp_act(a, it, n, 1, first)
                    if quad_done(n, FINISH_STEP - 2, first, tail):
                        copy_oT_act(a, it, n // GPQ - 1, first)
                    if n == OUT_STEP + 1 and not first:
                        a.wait_ge(obT_p, it)
                        a.copy(obT[:], bank[7][:]).then_inc(obT_d, 1)

            def body_dve(v, it, first, tail):
                for n in range(TAIL if tail else NG):
                    if runs(n, first, tail):
                        max_dve(v, it, n, 0)
                    if runs(n - W_LAG, first, tail):
                        recip_dve(v, it, n - W_LAG)
                    if runs(n, first, tail):
                        max_dve(v, it, n, 1)
                    if runs(n - W_LAG, first, tail):
                        coef_dve(v, it, n - W_LAG)
                    if not abs_on_act(n - ABS_LAG) and runs(n - ABS_LAG, first, tail):
                        abs_dve(v, it, n - ABS_LAG)
                    if runs(n - W_LAG, first, tail):
                        w_dve(v, it, n - W_LAG, first)
                    if quad_done(n, FINISH_STEP, first, tail):
                        finish_quad_dve(v, it, n // GPQ - 1, first)
                    if n == OUT_STEP + 3 and not first:
                        v.wait_ge(op_p, it)
                        xb = X[:, bass.ds((it - 1) * BPB, BPB), :]
                        v.tensor_tensor(xb, bank[7][:].rearrange("p (j d) -> p j d", d=D), xb, ALU.add).then_inc(x_d, 1)

            def body_sp(sp, it, first=False):
                for quad in range(QUADS):
                    s = quad % 2
                    if not (first and quad < 2):
                        sp.wait_ge(scored, nth(2 * NG, it, half((quad - 1) * GPQ - 1, 1)))
                    for t in range(3):
                        for par in range(2):
                            sp.dma_start(stack[64 * par:64 * par + ROWS, s, t, :, :],
                                         KD[t, bass.ds(it, 1), quad * 2 + par, :, :].rearrange("b (r h) n -> (b r) h n", h=2)
                                         ).then_inc(loaded[s], 16)

            def body_pool(pool, it, first):
                for quad in range(QUADS):
                    if not (first and quad < 2):
                        pool.wait_ge(av_d, nth(ROUNDS, it, (quad - 1) * len(ROUND_ENDS) - 1))
                    pool.tensor_copy(vq[:, quad % 2], V[:, bass.ds(it * BPB, BPB), quad * 32:(quad + 1) * 32]).then_inc(vq_d, 1)

            def sp_part(sp):
                over_batches(sp, proj_sp)
                for s in range(2):
                    sp.wait_ge(kd_out[s], 2 * 3 * TERMS * 16)
                body_sp(sp, 0, first=True)
                with sp.Fori(1, BATCH) as it:
                    body_sp(sp, it)

            def pool_part(pool):
                over_batches(pool, norm.pool)
                pool.wait_ge(v_d, BATCH)
                body_pool(pool, 0, True)
                with pool.Fori(1, BATCH) as it:
                    body_pool(pool, it, False)

            def dve_part(v):
                v.wait_ge(x_ready, BATCH)
                over_batches(v, proj_dve)
                steps(v, body_dve)

            def act_part(a):
                over_batches(a, proj_act)
                steps(a, body_act)

            def pe_part(pe):
                over_batches(pe, proj_pe)
                pe.wait_ge(v_d, BATCH)
                pe.wait_ge(res1, 3 * BATCH)
                steps(pe, body_pe)

            return dict(sp=sp_part, pool=pool_part, dve=dve_part, act=act_part, pe=pe_part), x_d

        def x_loaded(v):
            v.wait_ge(x_in, 16)

        ffn1, x1 = ffn("f1", x_loaded, False)
        attn, x2 = attention(x1)

        def x_attended(v):
            v.wait_ge(x2, BATCH)

        ffn2, _ = ffn("f2", x_attended, True)

        block = ctx.enter_context(nc.Block())

        @block.sync
        def _(sp):
            setup_sp(sp)
            ffn1["sp"](sp)
            attn["sp"](sp)
            ffn2["sp"](sp)

        @block.gpsimd
        def _(pool):
            setup_pool(pool)
            ffn1["pool"](pool)
            attn["pool"](pool)
            ffn2["pool"](pool)

        @block.vector
        def _(v):
            setup_dve(v)
            ffn1["dve"](v)
            attn["dve"](v)
            ffn2["dve"](v)

        @block.scalar
        def _(a):
            setup_act(a)
            ffn1["act"](a)
            attn["act"](a)
            ffn2["act"](a)

        @block.tensor
        def _(pe):
            setup_pe(pe)
            pe.wait_ge(dve_set, DVE_SET)
            ffn1["pe"](pe)
            attn["pe"](pe)
            ffn2["pe"](pe)


_INS = ["L0_attn_x", "L0_attn_Wq", "L0_attn_Wk1", "L0_attn_Wk2", "L0_attn_Wv", "L0_attn_Wo", "L0_attn_lambda_logit",
        "L0_ffn_wr", "L0_ffn_br", "L0_ffn_w1", "L0_ffn_b1", "L0_ffn_w2", "L0_ffn_b2"]


def kernel(**inputs):
    import numpy as _np
    import concourse.bacc as _bacc
    from concourse import mybir as _mybir
    from concourse.bass_utils import run_bass_kernel_spmd as _run

    nc = _bacc.Bacc("TRN2", target_bir_lowering=False, num_devices=1)
    arrays, args = {}, []
    for name in _INS:
        a = _np.ascontiguousarray(inputs[name])
        arrays[f"in_{name}_dram"] = a
        args.append(nc.dram_tensor(f"in_{name}_dram", a.shape, _mybir.dt.from_np(a.dtype), kind="ExternalInput").ap())
    out = nc.dram_tensor("out_0_dram", (BATCH, SEQ, D), _mybir.dt.float32, kind="ExternalOutput").ap()
    build(nc, *args, out)
    r = _run(nc, [arrays], core_ids=[0])
    return r.results[0]["out_0_dram"]
```

```python
from contextlib import ExitStack

import concourse.bass as bass
from concourse import mybir

ALU = mybir.AluOpType
ACT = mybir.ActivationFunctionType
AX = mybir.AxisListType
F32 = mybir.dt.float32
BF16 = mybir.dt.bfloat16
I32 = mybir.dt.int32
U32 = mybir.dt.uint32

P = 128
BATCH, SEQ, D = 4, 512, 128
NBLK = BATCH * SEQ // P
BPB = SEQ // P
HEADS, HD = 16, 8
E, F = 8, 512
FC = F // P
LN_EPS = 1e-5
SCALE = HD ** -0.5
DENOM_MIN = 1e-6
MASKED = -3.0e38

REGION = BATCH * SEQ + P
TILES = NBLK + E - 1
SPARE = E * REGION
PADS = E + TILES - NBLK
ROW = D + 1

Q_PARTS = [0, 0, 0, 1, 1, 2]
K_PARTS = [0, 1, 2, 0, 1, 0]
TERMS = len(Q_PARTS)
ROWS = TERMS * HD
QUADS = HEADS // 4

GROUPS_OF_QUAD = ([(3, [a]) for a in range(4)] + [(2, [a]) for a in range(4)]
                  + [(1, [0, 1]), (1, [2, 3])] + [(0, [0, 1, 2, 3])])
GPQ = len(GROUPS_OF_QUAD)
GROUPS = [(quad, i, heads) for quad in range(QUADS) for i, heads in GROUPS_OF_QUAD]
NG = len(GROUPS)
ROUND_ENDS = [g for g in range(GPQ) if g == GPQ - 1 or GROUPS_OF_QUAD[g][0] != GROUPS_OF_QUAD[g + 1][0]]
ROUNDS = len(ROUND_ENDS) * QUADS
W_SLOTS = 4
EX_SLOTS = 4
AV_PART = 2
W_LAG, ABS_LAG, TURN_LAG, AV_LAG = 2, 3, 4, 6
POOL_GROUPS = range(3, 8)
ABS_ON_ACT = 6
FINISH_STEP = 8


def nth(per, it, n):
    return it * per + (n + 1)


def build(nc, x, wq, wk1, wk2, wv, wo, lam, wr, br, w1, b1, w2, b2, out):
    with ExitStack() as ctx:
        def sb(name, shape, dt=F32):
            return ctx.enter_context(nc.sbuf_tensor(name, shape, dt))

        def sem(name):
            return ctx.enter_context(nc.semaphore(name))

        bank = [ctx.enter_context(nc.psum_tensor(f"bank{i}", [P, 512], F32)) for i in range(8)]

        X = sb("X", [P, NBLK, D])
        W1 = sb("W1", [P, E * F])
        W2 = sb("W2", [P, E * FC * D])
        WT = sb("WT", [P, 5, D])
        wraw = sb("wraw", [P, 5, D])
        wr_sb = sb("wr_sb", [P, E])
        br_sb = sb("br_sb", [P, E])
        B1S = sb("B1S", [3, E * F], BF16)
        B2S = sb("B2S", [3, E * D], BF16)
        ident = sb("ident", [P, P])
        identb = sb("identb", [P, P], BF16)
        maskb = sb("maskb", [P, P], BF16)
        trib = sb("trib", [P, P], BF16)
        onesb = sb("onesb", [P, P], BF16)
        padding = sb("padding", [P, PADS, ROW])
        number = sb("number", [P, NBLK])
        mhalf = sb("mhalf", [P, BPB])
        nlam = sb("nlam", [P, HEADS])
        lamt = sb("lamt", [P, 2, HEADS])
        em8 = sb("em8", [P, E])
        ereg = sb("ereg", [P, E])
        tri8 = sb("tri8", [P, E, E])
        iot = sb("iot", [P, TILES])
        iot128 = sb("iot128", [P, TILES])
        e9 = sb("e9", [P, E + 1])
        braw = sb("braw", [P, E * F // P + E * D // P])
        bres = sb("bres", [P, 2, E * F // P + E * D // P])
        bpart = sb("bpart", [P, 3, E * F // P + E * D // P], BF16)

        stats = sb("stats", [P, BATCH, BPB, 6])
        mv = sb("mv", [P, BATCH, BPB, 2])
        veps = sb("veps", [P, BATCH, BPB])
        rstd = sb("rstd", [P, BATCH, BPB])
        xn = sb("xn", [P, BATCH, BPB, ROW])
        xnT = sb("xnT", [P, BATCH, SEQ])
        rsc = sb("rsc", [P, BATCH, BPB, E])
        rmax = sb("rmax", [P, BATCH, BPB])
        req = sb("req", [P, BATCH, BPB, E])
        rcand = sb("rcand", [P, BATCH, BPB, E])
        rmin = sb("rmin", [P, BATCH, BPB])
        OH = sb("OH", [P, NBLK, E], BF16)
        seen = sb("seen", [P, E], BF16)
        seenf = sb("seenf", [P, BATCH, E])
        place = sb("place", [P, BATCH, BPB, E])
        slot = sb("slot", [P, BATCH, BPB])
        slotu = sb("slotu", [P, BATCH, BPB], U32)
        cnt = sb("cnt", [P, E])
        cnti = sb("cnti", [P, E], I32)
        ntile = sb("ntile", [P, E])
        ntilei = sb("ntilei", [P, E], I32)
        cprod = sb("cprod", [P, E, E])
        cend = sb("cend", [P, E])
        cstart = sb("cstart", [P, E])
        shift = sb("shift", [P, E])
        tge = sb("tge", [P, TILES, E])
        texp = sb("texp", [P, TILES])
        tone = sb("tone", [P, TILES, E + 1])
        trow = sb("trow", [P, TILES, E + 1])
        trowf = sb("trowf", [P, TILES])
        tilee = sb("tilee", [P, TILES], I32)
        tiler = sb("tiler", [P, TILES], I32)
        homes = sb("homes", [P, TILES])
        home = sb("home", [P, 4], U32)
        YG = sb("YG", [P, NBLK, D])

        tin = sb("tin", [P, 2, ROW])
        tinT = sb("tinT", [P, 2, P])
        hid = sb("hid", [P, 2, F])
        hidT = sb("hidT", [P, 2, FC, P])
        ytile = sb("ytile", [P, 4, D])

        V = sb("V", [P, NBLK, D])
        parts = sb("parts", [P, 3, 3, SEQ], BF16)
        resid = sb("resid", [P, 3, SEQ])
        stack = sb("stack", [P, 2, 3, 2, SEQ], BF16)
        negm = sb("negm", [P, 2, 2, 4])
        ex = sb("ex", [P, EX_SLOTS, 1024])
        w = sb("w", [P, W_SLOTS, 512])
        absw = sb("absw", [P, 512])
        wT = sb("wT", [P, 2, 4, 512])
        oT = sb("oT", [P, SEQ])
        Z = sb("Z", [P, 2, 16, 2])
        rz2 = sb("rz2", [P, 2, 4])
        ratio = sb("ratio", [P, 2, 4])
        coef = sb("coef", [P, W_SLOTS, 4])
        e2c = sb("e2c", [P, SEQ])
        asum = sb("asum", [P, 2, 16])
        den = sb("den", [P, 2, 16])
        rden = sb("rden", [P, 2, 16])
        vq = sb("vq", [P, 2, BPB, 32])
        ob = sb("ob", [P, BPB, D])
        obT = sb("obT", [P, SEQ])

        XS = nc.dram_tensor("rows_by_expert", [SPARE + TILES * P, ROW], F32, kind="Internal").ap()
        YT = nc.dram_tensor("rows_by_token", [BATCH * SEQ + PADS * P, D], F32, kind="Internal").ap()
        KD = nc.dram_tensor("stacks", [3, BATCH, TERMS, D, SEQ], BF16, kind="Internal").ap()

        x_in = [sem(f"x_in{b}") for b in range(BATCH)]
        small_in = sem("small_in")
        w1_in = sem("w1_in")
        w2_in = sem("w2_in")
        pool_set = sem("pool_set")
        dve_set = sem("dve_set")
        act_set = sem("act_set")
        pe_set = sem("pe_set")
        bias_in = sem("bias_in")
        spare_zero = sem("spare_zero")
        out_stored = sem("out_stored")

        NSET_POOL = 18

        def setup_sp(sp):
            for b in range(BATCH):
                sp.dma_start(X[:, b * BPB:(b + 1) * BPB, :], x[b].rearrange("(t p) d -> p t d", p=P)).then_inc(x_in[b], 16)
            for t, src in enumerate((wq, wk1, wk2, wv, wo)):
                sp.dma_start(wraw[:, t, :], src).then_inc(small_in, 16)
            sp.dma_start(wr_sb[:], wr).then_inc(small_in, 16)
            sp.dma_start(br_sb[:], br.rearrange("(a e) -> a e", a=1).to_broadcast([P, E])).then_inc(small_in, 16)
            sp.dma_start(lamt[:, 0, :], lam.rearrange("(a e) -> a e", a=1).to_broadcast([P, HEADS])).then_inc(small_in, 16)
            sp.dma_start(braw[:, 0:E * F // P], b1.rearrange("e (a f) -> (e a) f", a=P // E)).then_inc(small_in, 16)
            sp.dma_start(braw[:, E * F // P:], b2.rearrange("e (a f) -> (e a) f", a=P // E)).then_inc(small_in, 16)
            sp.dma_start(W1[:].rearrange("p (e f) -> p e f", e=E), w1.rearrange("e h f -> h e f")).then_inc(w1_in, 16)
            sp.dma_start(W2[:].rearrange("p (e c h) -> p e c h", e=E, c=FC),
                         w2.rearrange("e (c p) h -> p e c h", p=P)).then_inc(w2_in, 16)
            sp.wait_ge(dve_set, DVE_BIASES)
            for k in range(3):
                sp.dma_start(B1S[k:k + 1, :], bpart[:, k, 0:E * F // P]).then_inc(bias_in, 16)
                sp.dma_start(B2S[k:k + 1, :], bpart[:, k, E * F // P:]).then_inc(bias_in, 16)
            sp.wait_ge(pool_set, NSET_POOL)
            sp.dma_start(XS[SPARE:SPARE + (PADS - E) * P, :].rearrange("(k p) d -> p k d", p=P), padding[:, E:, :]).then_inc(spare_zero, 16)

        def setup_pool(pool):
            n = [0]

            def step(ins):
                n[0] += 1
                return ins.then_inc(pool_set, 1)

            step(pool.memset(ident[:], 0.0))
            step(pool.memset(maskb[:], 0.0))
            step(pool.memset(onesb[:], 1.0))
            step(pool.memset(tri8[:], 1.0))
            step(pool.memset(padding[:, :, 0:D], 0.0))
            step(pool.memset(mhalf[:], -0.5))
            pool.wait_ge(pool_set, n[0])
            step(pool.affine_select(out=ident[:], in_=ident[:], compare_op=ALU.not_equal, fill=1.0, base=0,
                                    pattern=[[-1, P]], channel_multiplier=1))
            step(pool.affine_select(out=maskb[:], in_=maskb[:], compare_op=ALU.is_ge, fill=MASKED, base=0,
                                    pattern=[[-1, P]], channel_multiplier=1))
            step(pool.affine_select(out=trib[:], in_=onesb[:], compare_op=ALU.is_gt, fill=0.0, base=0,
                                    pattern=[[1, P]], channel_multiplier=-1))
            step(pool.affine_select(out=tri8[:], in_=tri8[:], compare_op=ALU.is_ge, fill=0.0, base=0,
                                    pattern=[[1, E], [-1, E]], channel_multiplier=0))
            step(pool.iota(number[:], pattern=[[P, NBLK]], base=0, channel_multiplier=1,
                           allow_small_or_imprecise_dtypes=True))
            step(pool.iota(padding[:, :, D:ROW], pattern=[[P, PADS], [0, 1]], base=BATCH * SEQ, channel_multiplier=1,
                           allow_small_or_imprecise_dtypes=True))
            step(pool.iota(trow[:, :, E:E + 1], pattern=[[-P, TILES], [0, 1]], base=SPARE + (TILES - 1) * P,
                           channel_multiplier=0, allow_small_or_imprecise_dtypes=True))
            for t, base, k, m in ((em8, -8, 1, E), (ereg, 0, REGION, E), (e9, 0, 1, E + 1), (iot, 0, 1, TILES),
                                  (iot128, 0, P, TILES)):
                step(pool.iota(t[:], pattern=[[k, m]], base=base, channel_multiplier=0,
                               allow_small_or_imprecise_dtypes=True))
            assert n[0] == NSET_POOL

        def setup_biases_dve(v):
            v.wait_ge(small_in, 16 * 10)
            v.tensor_copy(bpart[:, 0, :], braw[:]).then_inc(dve_set, 1)
            v.wait_ge(dve_set, 1)
            v.tensor_tensor(bres[:, 0, :], braw[:], bpart[:, 0, :], ALU.subtract).then_inc(dve_set, 1)
            v.wait_ge(dve_set, 2)
            v.tensor_copy(bpart[:, 1, :], bres[:, 0, :]).then_inc(dve_set, 1)
            v.wait_ge(dve_set, 3)
            v.tensor_tensor(bpart[:, 2, :], bres[:, 0, :], bpart[:, 1, :], ALU.subtract).then_inc(dve_set, 1)

        def setup_dve(v):
            v.wait_ge(pool_set, NSET_POOL)
            v.tensor_copy(identb[:], ident[:]).then_inc(dve_set, 1)
            v.wait_ge(act_set, 1)
            v.tensor_scalar(lamt[:, 0, :], lamt[:, 1, :], 1.0, -1.0, ALU.add, ALU.mult).then_inc(dve_set, 1)
            v.wait_ge(dve_set, 6)
            v.reciprocal(nlam[:], lamt[:, 0, :]).then_inc(dve_set, 1)
            v.wait_ge(pe_set, 1)
            for t in range(3):
                v.tensor_copy(WT[:, t, :].rearrange("k (g d h) -> k g d h", h=2, d=HD),
                              bank[0][:, t * D:(t + 1) * D].rearrange("k (g h d) -> k g d h", h=2, d=HD)).then_inc(dve_set, 1)
            v.tensor_copy(WT[:, 3, :], bank[0][:, 3 * D:4 * D]).then_inc(dve_set, 1)
            v.tensor_copy(WT[:, 4, :], bank[1][:, 0:D]).then_inc(dve_set, 1)

        def setup_act(a):
            a.wait_ge(small_in, 16 * 10)
            a.activation(lamt[:, 1, :], lamt[:, 0, :], ACT.Exp, scale=-1.0).then_inc(act_set, 1)

        def setup_pe(pe):
            pe.wait_ge(small_in, 16 * 10)
            pe.wait_ge(pool_set, NSET_POOL)
            for t in range(5):
                last = pe.transpose(bank[t // 4][:, (t % 4) * D:(t % 4 + 1) * D], wraw[:, t, :], ident[:])
            last.then_inc(pe_set, 1)

        DVE_BIASES, DVE_SET = 4, 12

        waits_passed = sem("waits_passed")

        def alone(eng):
            eng.sem_inc(waits_passed, 1)

        class Norm:

            def __init__(self, tag, banks):
                self.banks = banks
                self.stat = sem(f"{tag}_stat")
                self.mv = sem(f"{tag}_mv")
                self.veps = sem(f"{tag}_veps")
                self.rstd = sem(f"{tag}_rstd")
                self.xn = sem(f"{tag}_xn")
                self.tr = sem(f"{tag}_tr")
                self.xnT = sem(f"{tag}_xnT")

            def dve_stats(self, v, b, s):
                for j in range(BPB):
                    v.bn_stats(stats[:, s, j, :], X[:, bass.ds(b * BPB + j, 1), :]).then_inc(self.stat, 1)
                v.wait_ge(self.stat, (b + 1) * BPB)
                alone(v)
                for j in range(BPB):
                    ins = v.bn_aggr(mv[:, s, j, :], stats[:, s, j, :])
                ins.then_inc(self.mv, 1)

            def pool(self, pool, b, s):
                pool.wait_ge(self.mv, b + 1)
                alone(pool)
                pool.tensor_scalar(veps[:, s, :], mv[:, s, :, 1], LN_EPS, None, ALU.add).then_inc(self.veps, 1)
                pool.wait_ge(self.veps, b + 1)
                alone(pool)
                pool.tensor_tensor(rstd[:, s, :], veps[:, s, :], mhalf[:], ALU.pow).then_inc(self.rstd, 1)

            def dve_apply(self, v, b, s):
                v.wait_ge(self.rstd, b + 1)
                for j in range(BPB):
                    ins = v.tensor_scalar(xn[:, s, j, 0:D], X[:, bass.ds(b * BPB + j, 1), :], mv[:, s, j, 0:1],
                                          rstd[:, s, j:j + 1], ALU.subtract, ALU.mult)
                ins.then_inc(self.xn, 1)

            def pe(self, pe, b, s):
                pe.wait_ge(self.xn, b + 1)
                for j in range(BPB):
                    ins = pe.transpose(self.banks[s][:, j * P:(j + 1) * P], xn[:, s, j, 0:D], ident[:])
                ins.then_inc(self.tr, 1)

            def act(self, a, b, s):
                a.wait_ge(self.tr, b + 1)
                a.copy(xnT[:, s, :], self.banks[s][:]).then_inc(self.xnT, 1)

        class Routing:
            def __init__(self, tag, t_banks, s_banks, r_banks):
                self.norm = Norm(tag, t_banks)
                self.s_banks, self.r_banks = s_banks, r_banks
                self.score = sem(f"{tag}_score")
                self.rsc = sem(f"{tag}_rsc")
                self.rmax = sem(f"{tag}_rmax")
                self.req = sem(f"{tag}_req")
                self.cand = sem(f"{tag}_cand")
                self.rmin = sem(f"{tag}_rmin")
                self.oh = sem(f"{tag}_oh")
                self.rank = sem(f"{tag}_rank")
                self.sum = sem(f"{tag}_sum")
                self.seen = sem(f"{tag}_seen")
                self.place = sem(f"{tag}_place")
                self.picked = sem(f"{tag}_picked")
                self.slot = sem(f"{tag}_slot")
                self.slotu = sem(f"{tag}_slotu")
                self.numbered = sem(f"{tag}_numbered")
                self.scattered = [sem(f"{tag}_scattered{s}") for s in range(BATCH)]

            def start_dve(self, v):
                v.memset(seen[:], 0.0).then_inc(self.seen, 1)

            def score_pe(self, pe, b, s):
                pe.wait_ge(self.norm.xnT, b + 1)
                for j in range(BPB):
                    ins = pe.matmul(self.s_banks[s][:, j * E:(j + 1) * E], xnT[:, s, j * P:(j + 1) * P], wr_sb[:],
                                    start=True, stop=True)
                ins.then_inc(self.score, 1)

            def score_dve(self, v, b, s):
                v.wait_ge(self.score, b + 1)
                v.tensor_tensor(rsc[:, s], self.s_banks[s][:, 0:BPB * E].rearrange("p (j e) -> p j e", e=E),
                                br_sb[:].rearrange("p (a e) -> p a e", a=1).to_broadcast([P, BPB, E]), ALU.add).then_inc(self.rsc, 1)

            def max_dve(self, v, b, s):
                v.wait_ge(self.rsc, b + 1)
                v.tensor_reduce(rmax[:, s, :], rsc[:, s], AX.X, ALU.max).then_inc(self.rmax, 1)

            def equal_dve(self, v, b, s):
                v.wait_ge(self.rmax, b + 1)
                v.tensor_tensor(req[:, s], rsc[:, s], over_e(rmax[:, s, :]), ALU.is_equal).then_inc(self.req, 1)

            def cand_dve(self, v, b, s):
                v.wait_ge(self.req, b + 1)
                v.tensor_tensor(rcand[:, s], req[:, s], over_blocks(em8), ALU.mult).then_inc(self.cand, 1)

            def min_dve(self, v, b, s):
                v.wait_ge(self.cand, b + 1)
                v.tensor_reduce(rmin[:, s, :], rcand[:, s], AX.X, ALU.min).then_inc(self.rmin, 1)

            def onehot_dve(self, v, b, s):
                v.wait_ge(self.rmin, b + 1)
                v.tensor_tensor(OH[:, bass.ds(b * BPB, BPB), :], over_blocks(em8), over_e(rmin[:, s, :]), ALU.is_equal).then_inc(self.oh, 1)

            def sum_dve(self, v, b, s):
                v.wait_ge(self.oh, b + 1)
                alone(v)
                v.tensor_reduce(seenf[:, s, :], OH[:, bass.ds(b * BPB, BPB), :].rearrange("p j e -> p e j"), AX.X, ALU.add).then_inc(self.sum, 1)

            def rank_pe(self, pe, b, s):
                pe.wait_ge(self.oh, b + 1)
                pe.wait_ge(self.seen, b + 1)
                r = self.r_banks[s][:, 0:BPB * E].rearrange("p (j e) -> p j e", e=E)
                pe.matmul(r, onesb[:], seen[:].rearrange("p (a e) -> p a e", a=1).to_broadcast([P, BPB, E]),
                          start=True, stop=False, skip_group_check=True)
                for j in range(BPB - 1):
                    pe.matmul(r[:, j + 1:, :], onesb[:], OH[:, bass.ds(b * BPB + j, 1), :].to_broadcast([P, BPB - 1 - j, E]),
                              start=False, stop=False, skip_group_check=True)
                pe.matmul(r, trib[:], OH[:, bass.ds(b * BPB, BPB), :], start=False, stop=True,
                          skip_group_check=True).then_inc(self.rank, 1)

            def place_dve(self, v, b, s):
                v.wait_ge(self.rank, b + 1)
                v.tensor_tensor(place[:, s], self.r_banks[s][:, 0:BPB * E].rearrange("p (j e) -> p j e", e=E),
                                over_blocks(ereg), ALU.add).then_inc(self.place, 1)

            def seen_dve(self, v, b, s):
                v.wait_ge(self.sum, b + 1)
                v.tensor_tensor(seen[:], seen[:], seenf[:, s, :], ALU.add).then_inc(self.seen, 1)

            def picked_dve(self, v, b, s):
                v.wait_ge(self.place, b + 1)
                v.tensor_tensor(place[:, s], place[:, s], OH[:, bass.ds(b * BPB, BPB), :], ALU.mult).then_inc(self.picked, 1)

            def slot_dve(self, v, b, s):
                v.wait_ge(self.picked, b + 1)
                v.tensor_reduce(slot[:, s, :], place[:, s], AX.X, ALU.add).then_inc(self.slot, 1)

            def slotu_dve(self, v, b, s):
                v.wait_ge(self.slot, b + 1)
                v.tensor_copy(slotu[:, s, :], slot[:, s, :]).then_inc(self.slotu, 1)

            def scatter_pool(self, pool, b, s):
                pool.wait_ge(self.slotu, b + 1)
                alone(pool)
                pool.tensor_copy(xn[:, s, :, D], number[:, bass.ds(b * BPB, BPB)]).then_inc(self.numbered, 1)
                pool.wait_ge(self.numbered, b + 1)
                alone(pool)
                for j in range(BPB):
                    pool.indirect_dma_start(out=XS, out_offset=bass.IndirectOffsetOnAxis(ap=slotu[:, s, j:j + 1], axis=0),
                                            in_=xn[:, s, j, :], in_offset=None).then_inc(self.scattered[s], 16)

        def over_e(t):
            return t.rearrange("p (j a) -> p j a", a=1).to_broadcast([P, BPB, E])

        def over_blocks(t):
            return t[:].rearrange("p (a e) -> p a e", a=1).to_broadcast([P, BPB, E])

        def ffn(tag, routing, scatters, store):
            count_p = sem(f"{tag}_count")
            table = sem(f"{tag}_table")
            padded = sem(f"{tag}_padded")
            tin_in = [sem(f"{tag}_tin{s}") for s in range(2)]
            tinT_p = sem(f"{tag}_tinT_p")
            tinT_d = sem(f"{tag}_tinT")
            hid_p = sem(f"{tag}_hid_p")
            hid_d = sem(f"{tag}_hid")
            hidT_p = sem(f"{tag}_hidT_p")
            hidT_d = sem(f"{tag}_hidT")
            y_p = sem(f"{tag}_y_p")
            y_d = sem(f"{tag}_y")
            home_d = sem(f"{tag}_home")
            homeu_d = sem(f"{tag}_homeu")
            y_out = [sem(f"{tag}_y_out{s}") for s in range(4)]
            gathered = [sem(f"{tag}_gathered{b}") for b in range(BATCH)]
            x_d = sem(f"{tag}_x")

            def table_dve(v):
                n = [0]

                def step(ins):
                    ins.then_inc(table, 1)
                    n[0] += 1
                    v.wait_ge(table, n[0])

                def mid(t, k, m):
                    return t.rearrange("p (a e) -> p a e", a=1).to_broadcast([P, k, m])

                def last(t, k, m):
                    return t.rearrange("p (j a) -> p j a", a=1).to_broadcast([P, k, m])

                v.wait_ge(count_p, 1)
                step(v.tensor_copy(cnt[:], bank[6][:, 0:E]))
                step(v.tensor_copy(cnti[:], cnt[:]))
                step(v.tensor_scalar(ntile[:], cnt[:], 1.0 / P, (P - 1) / (2.0 * P), ALU.mult, ALU.add))
                step(v.tensor_copy(ntilei[:], ntile[:]))
                step(v.tensor_copy(ntile[:], ntilei[:]))
                step(v.tensor_tensor(cprod[:], tri8[:], mid(ntile[:], E, E), ALU.mult))
                step(v.tensor_reduce(cend[:], cprod[:], AX.X, ALU.add))
                step(v.tensor_tensor(cstart[:], cend[:], ntile[:], ALU.subtract))
                step(v.scalar_tensor_tensor(out=shift[:], in0=cstart[:], scalar=-float(P), in1=ereg[:],
                                            op0=ALU.mult, op1=ALU.add))
                step(v.tensor_tensor(tge[:], last(iot[:], TILES, E), mid(cend[:], TILES, E), ALU.is_ge))
                step(v.tensor_reduce(texp[:], tge[:], AX.X, ALU.add))
                step(v.tensor_tensor(tone[:], last(texp[:], TILES, E + 1), mid(e9[:], TILES, E + 1), ALU.is_equal))
                step(v.tensor_tensor(trow[:, :, 0:E], last(iot128[:], TILES, E), mid(shift[:], TILES, E), ALU.add))
                step(v.tensor_tensor(tone[:], tone[:], trow[:], ALU.mult))
                step(v.tensor_reduce(trowf[:], tone[:], AX.X, ALU.add))
                step(v.tensor_copy(tiler[:], trowf[:]))
                step(v.tensor_scalar(tilee[:], texp[:], float(E - 1), None, ALU.min))
                assert n[0] == TABLE

            TABLE, TABLE_COUNTS = 17, 2

            def load_tile(sp, t, s):
                if not (isinstance(t, int) and t < 2):
                    sp.wait_ge(tinT_p, t - 1)
                    sp.wait_ge(home_d, t - 1)
                row = sp.value_load(tiler[0:1, bass.ds(t, 1)], min_val=0, max_val=SPARE + (TILES - 1) * P)
                sp.dma_start(tin[:, s, :], XS[bass.ds(row, P), :]).then_inc(tin_in[s], 16)

            def turn_in(pe, t, s):
                pe.wait_ge(tin_in[s], (t // 2 + 1) * 16 if isinstance(t, int) else (t - s) * 8 + 16)
                if not (isinstance(t, int) and t < 2):
                    pe.wait_ge(tinT_d, t - 1)
                pe.transpose(bank[s][:, 0:P], tin[:, s, 0:D], ident[:]).then_inc(tinT_p, 1)

            def up(pe, t, s):
                e = pe.value_load(tilee[0:1, bass.ds(t, 1)], min_val=0, max_val=E - 1)
                if not (isinstance(t, int) and t < 2):
                    pe.wait_ge(hid_d, t - 1)
                pe.matmul(bank[2 + s][:], onesb[0:3, :], B1S[:, bass.ds(e * F, F)], start=True, stop=False)
                pe.wait_ge(tinT_d, t + 1)
                pe.matmul(bank[2 + s][:], tinT[:, s, :], W1[:, bass.ds(e * F, F)],
                          start=False, stop=True).then_inc(hid_p, 1)

            def turn_hidden(pe, t, s):
                pe.wait_ge(hid_d, t + 1)
                if not (isinstance(t, int) and t < 2):
                    pe.wait_ge(hidT_d, t - 1)
                for c in range(FC):
                    ins = pe.transpose(bank[4 + s][:, c * P:(c + 1) * P], hid[:, s, c * P:(c + 1) * P], ident[:])
                ins.then_inc(hidT_p, 1)

            def down(pe, t, s):
                e = pe.value_load(tilee[0:1, bass.ds(t, 1)], min_val=0, max_val=E - 1)
                if not (isinstance(t, int) and t < 2):
                    pe.wait_ge(y_d, t - 1)
                pe.matmul(bank[6 + s][:, 0:D], onesb[0:3, :], B2S[:, bass.ds(e * D, D)], start=True, stop=False)
                pe.wait_ge(hidT_d, t + 1)
                for c in range(FC):
                    ins = pe.matmul(bank[6 + s][:, 0:D], hidT[:, s, c, :], W2[:, bass.ds(e * (FC * D) + c * D, D)],
                                    start=False, stop=c == FC - 1)
                ins.then_inc(y_p, 1)

            def over_tiles(eng, step):
                quads = TILES // 4
                for t in range(8):
                    step(eng, t, t % 4)
                with eng.Fori(2, quads) as q4:
                    for s in range(4):
                        step(eng, q4 * 4 + s, s)
                for t in range(quads * 4, TILES + 2):
                    step(eng, t, t % 4)

            def known(t, lo, hi):
                return not isinstance(t, int) or lo <= t < hi

            def tile_pe(pe, t, s4):
                s = s4 % 2
                if known(t, 0, TILES):
                    up(pe, t, s)
                if known(t, 1, TILES + 1):
                    turn_hidden(pe, t - 1, 1 - s)
                if known(t, 0, TILES - 1):
                    turn_in(pe, t + 1, 1 - s)
                if known(t, 2, TILES + 2):
                    down(pe, t - 2, s)

            def tile_act(a, t, s4):
                s, y4 = s4 % 2, (s4 + 2) % 4
                if known(t, 0, TILES):
                    a.wait_ge(hid_p, t + 1)
                    if not (isinstance(t, int) and t < 2):
                        a.wait_ge(hidT_p, t - 1)
                    a.activation(hid[:, s, :], bank[2 + s][:], ACT.Gelu).then_inc(hid_d, 1)
                if known(t, 2, TILES + 2):
                    a.wait_ge(y_p, t - 1)
                    if not (isinstance(t, int) and t < 6):
                        a.wait_ge(y_out[y4], (t - 2) // 4 * 16 if isinstance(t, int) else (t - 2 - y4) * 4)
                    a.copy(ytile[:, y4, :], bank[6 + s][:, 0:D]).then_inc(y_d, 1)

            def give_back_pool(pool, t, s4):
                pool.wait_ge(home_d, t + 1)
                if not (isinstance(t, int) and t < 4):
                    pool.wait_ge(y_out[s4], t // 4 * 16 if isinstance(t, int) else (t - s4) * 4)
                alone(pool)
                pool.tensor_copy(home[:, s4:s4 + 1], homes[:, bass.ds(t, 1)]).then_inc(homeu_d, 1)
                pool.wait_ge(homeu_d, t + 1)
                pool.wait_ge(y_d, t + 1)
                alone(pool)
                pool.indirect_dma_start(out=YT, out_offset=bass.IndirectOffsetOnAxis(ap=home[:, s4:s4 + 1], axis=0),
                                        in_=ytile[:, s4, :], in_offset=None).then_inc(y_out[s4], 16)

            def tile_dve(v, t, s4):
                s = s4 % 2
                if known(t, 0, TILES - 1):
                    v.wait_ge(tinT_p, t + 2)
                    if not (isinstance(t, int) and t < 1):
                        v.wait_ge(hid_p, t)
                    v.tensor_copy(tinT[:, 1 - s, :], bank[1 - s][:, 0:P]).then_inc(tinT_d, 1)
                    v.tensor_copy(homes[:, bass.ds(t + 1, 1)], tin[:, 1 - s, D:ROW]).then_inc(home_d, 1)
                if known(t, 1, TILES + 1):
                    v.wait_ge(hidT_p, t)
                    if not (isinstance(t, int) and t < 3):
                        v.wait_ge(y_p, t - 2)
                    v.tensor_copy(hidT[:, 1 - s].rearrange("p c k -> p (c k)"), bank[4 + 1 - s][:]).then_inc(hidT_d, 1)

            def pad(eng, experts):
                eng.wait_ge(table, TABLE_COUNTS)
                for e in experts:
                    n = eng.value_load(cnti[0:1, e:e + 1], min_val=0, max_val=BATCH * SEQ)
                    eng.dma_start(XS[bass.ds(n + e * REGION, P), :], padding[:, e, :]).then_inc(padded, 16)

            def sp_part(sp):
                pad(sp, range(0, E, 2))
                sp.wait_ge(table, TABLE)
                sp.wait_ge(padded, 16 * E)
                sp.wait_ge(spare_zero, 16)
                for s in range(BATCH):
                    if scatters[s]:
                        sp.wait_ge(routing.scattered[s], 16 * scatters[s])
                for t in range(2):
                    load_tile(sp, t, t)
                with sp.Fori(1, (TILES - 1) // 2) as pair:
                    for s in range(2):
                        load_tile(sp, pair * 2 + s, s)
                load_tile(sp, TILES - 1, (TILES - 1) % 2)
                for s in range(4):
                    sp.wait_ge(y_out[s], 16 * ((TILES + 3 - s) // 4))
                for b in range(BATCH):
                    sp.dma_start(YG[:, b * BPB:(b + 1) * BPB, :],
                                 YT[b * SEQ:(b + 1) * SEQ, :].rearrange("(t p) d -> p t d", p=P)).then_inc(gathered[b], 16)
                if store:
                    for b in range(BATCH):
                        sp.wait_ge(x_d, b + 1)
                        sp.dma_start(out[b].rearrange("(t p) d -> p t d", p=P), X[:, b * BPB:(b + 1) * BPB, :]).then_inc(out_stored, 16)
                    sp.wait_ge(out_stored, 16 * BATCH)

            def pool_part(pool):
                quads = TILES // 4
                for t in range(4):
                    give_back_pool(pool, t, t)
                with pool.Fori(1, quads) as q4:
                    for s in range(4):
                        give_back_pool(pool, q4 * 4 + s, s)
                for t in range(quads * 4, TILES):
                    give_back_pool(pool, t, t % 4)

            def dve_part(v):
                table_dve(v)
                v.wait_ge(tinT_p, 1)
                v.tensor_copy(tinT[:, 0, :], bank[0][:, 0:P]).then_inc(tinT_d, 1)
                v.tensor_copy(homes[:, 0:1], tin[:, 0, D:ROW]).then_inc(home_d, 1)
                over_tiles(v, tile_dve)
                for b in range(BATCH):
                    v.wait_ge(gathered[b], 16)
                    xb = X[:, b * BPB:(b + 1) * BPB, :]
                    v.scalar_tensor_tensor(out=xb, in0=YG[:, b * BPB:(b + 1) * BPB, :], scalar=0.5, in1=xb,
                                           op0=ALU.mult, op1=ALU.add).then_inc(x_d, 1)

            def act_part(a):
                pad(a, range(1, E, 2))
                over_tiles(a, tile_act)

            def pe_part(pe):
                pe.wait_ge(routing.seen, BATCH + 1)
                pe.matmul(bank[6][:, 0:E], onesb[:], seen[:], start=True, stop=True).then_inc(count_p, 1)
                pe.wait_ge(table, TABLE)
                pe.wait_ge(w1_in, 16)
                pe.wait_ge(w2_in, 16)
                pe.wait_ge(bias_in, 16 * 6)
                turn_in(pe, 0, 0)
                over_tiles(pe, tile_pe)

            return dict(sp=sp_part, pool=pool_part, dve=dve_part, act=act_part, pe=pe_part), x_d

        def attention(x_ready, routing):
            norm = Norm("at", [bank[7]])
            proj = sem("at_proj")
            vproj = sem("at_vproj")
            high = sem("at_high")
            res1 = sem("at_res1")
            middle = sem("at_middle")
            low = sem("at_low")
            v_d = sem("at_v")
            kd_out = sem("at_kd_out")
            loaded = [sem(f"at_loaded{s}") for s in range(2)]
            scored = sem("at_scored")
            maxed = sem("at_maxed")
            exped = sem("at_exped")
            rz_d = sem("at_rz")
            ratio_d = sem("at_ratio")
            coef_d = sem("at_coef")
            w_v = sem("at_w")
            w_p = sem("at_w_pool")
            e2c_d = sem("at_e2c")
            asum_d = sem("at_asum")
            turned = sem("at_turned")
            wT_d = sem("at_wT")
            av_d = sem("at_av")
            vq_d = sem("at_vq")
            asum_a = sem("at_asum_a")
            oT_d = sem("at_oT")
            back = sem("at_back")
            den_d = sem("at_den")
            rden_d = sem("at_rden")
            ob_d = sem("at_ob")
            obT_p = sem("at_obT_p")
            obT_d = sem("at_obT")
            op_p = sem("at_op_p")
            x_d = sem("at_x")

            def later(b):
                return not (isinstance(b, int) and b == 0)

            scales = (SCALE, 1.0, 1.0)

            def proj_pe(pe, b, t, o=bank[7]):
                pe.wait_ge(norm.xnT, b + 1)
                pe.matmul(o[:], WT[:, t, :], xnT[:, 0, :], start=True, stop=True).then_inc(proj, 1)

            def v_pe(pe, b, o=bank[7]):
                for j in range(BPB):
                    ins = pe.matmul(o[:, j * P:(j + 1) * P], xnT[:, 0, j * P:(j + 1) * P], WT[:, 3, :], start=True, stop=True)
                ins.then_inc(vproj, 1)

            def high_act(a, b, t, o=bank[7]):
                if t == 0 and later(b):
                    a.wait_ge(kd_out, b * (3 * 3 * 16))
                a.wait_ge(proj, 3 * b + (t + 1))
                a.mul(parts[:, t, 0, :], o[:], scales[t]).then_inc(high, 1)

            def rest_dve(v, b, t, o=bank[7]):
                v.wait_ge(high, 3 * b + (t + 1))
                if later(b):
                    v.wait_ge(middle, 3 * b + (t - 2))
                v.scalar_tensor_tensor(out=resid[:, t, :], in0=o[:], scalar=scales[t], in1=parts[:, t, 0, :],
                                       op0=ALU.mult, op1=ALU.subtract).then_inc(res1, 1)

            def middle_act(a, b, t):
                a.wait_ge(res1, 3 * b + (t + 1))
                a.copy(parts[:, t, 1, :], resid[:, t, :]).then_inc(middle, 1)

            def low_dve(v, b, t):
                v.wait_ge(middle, 3 * b + (t + 1))
                v.tensor_tensor(parts[:, t, 2, :], resid[:, t, :], parts[:, t, 1, :], ALU.subtract).then_inc(low, 1)

            def v_act(a, b, o=bank[7]):
                a.wait_ge(vproj, b + 1)
                a.copy(V[:, bass.ds(b * BPB, BPB), :], o[:].rearrange("p (j d) -> p j d", d=D)).then_inc(v_d, 1)

            def store_sp(sp, b, t):
                sp.wait_ge(low, 3 * b + (t + 1))
                term = 0
                for n in (3, 2, 1):
                    src = (parts[:, t, 3 - n, :].rearrange("p (a n) -> p a n", a=1).to_broadcast([P, n, SEQ]) if t == 0
                           else parts[:, t, 0:n, :])
                    sp.dma_start(KD[t, bass.ds(b, 1), term:term + n, :, :].rearrange("b m r n -> r (b m) n"), src).then_inc(kd_out, 16)
                    term += n

            def spot(i, k, st):
                return (2 * k + st) * (i + 1) * P if i < 2 else st * 512

            def s_ap(n, i, k, st, lo=0, hi=None):
                width = (i + 1) * P
                at = spot(i, k, st)
                b = bank[2 * (n % 2) + at // 512]
                return b[:, at % 512 + lo:at % 512 + (width if hi is None else hi)]

            def ex_ap(n, i, k, st):
                return ex[:, n % EX_SLOTS, spot(i, k, st):spot(i, k, st) + (i + 1) * P]

            def bank_items(n, h):
                _, i, heads = GROUPS[n]
                return [(k, st) for k in range(len(heads)) for st in range(2) if spot(i, k, st) // 512 == h]

            def half(n, h):
                return 2 * n + h

            def round_of(n):
                return n // GPQ * len(ROUND_ENDS) + (3 - GROUPS[n % NG][1])

            def starts_round(n):
                return n % GPQ == 0 or (n % GPQ - 1) in ROUND_ENDS

            def abs_on_act(n):
                return n % GPQ < ABS_ON_ACT

            ACT_SUMS = sum(abs_on_act(n) for n in range(GPQ))
            DVE_SUMS = GPQ - ACT_SUMS

            def on_pool(n):
                return n % GPQ in POOL_GROUPS

            def w_index(n):
                same = [g for g in range(GPQ) if on_pool(g) == on_pool(n)]
                return n // GPQ * len(same) + same.index(n % GPQ)

            def wait_w(eng, it, n):
                if on_pool(n):
                    eng.wait_ge(w_p, nth(len(POOL_GROUPS) * QUADS, it, w_index(n)))
                else:
                    eng.wait_ge(w_v, nth((GPQ - len(POOL_GROUPS)) * QUADS, it, w_index(n)))

            def scores_pe(pe, it, n, first):
                quad, i, heads = GROUPS[n]
                slot = quad % 2
                if n % GPQ == 0:
                    pe.wait_ge(loaded[slot], (it * 2 + quad // 2 + 1) * (6 * 16))
                per_bank = (2 if i == 1 else 4) if i < 2 else 1
                for h in range(2):
                    if not (first and n < 2):
                        pe.wait_ge(exped, nth(2 * NG, it, half(n - 2, h)))
                    o = bank[2 * (n % 2) + h][:, 0:per_bank * (i + 1) * P].rearrange("p (m c) -> p m c", m=per_bank)[:, :, i * P:]
                    pe.matmul(o, identb[:], maskb[:].rearrange("p (a c) -> p a c", a=1).to_broadcast([P, per_bank, P]),
                              start=True, stop=False, skip_group_check=True)
                    for k, st in bank_items(n, h):
                        a = heads[k]
                        r = slice(64 * (a // 2), 64 * (a // 2) + ROWS)
                        ins = pe.matmul(s_ap(n, i, k, st), stack[r, slot, 0, a % 2, i * P:(i + 1) * P],
                                        stack[r, slot, 1 + st, a % 2, 0:(i + 1) * P],
                                        start=False, stop=True, skip_group_check=True)
                    ins.then_inc(scored, 1)

            def turn_pe(pe, it, n, first):
                _, i, heads = GROUPS[n % NG]
                wait_w(pe, it, n)
                if not (first and n < 2):
                    pe.wait_ge(wT_d, nth(NG, it, n - 2))
                for c in range(len(heads) * (i + 1)):
                    ins = pe.transpose(bank[4 + n % 2][:, c * P:(c + 1) * P], w[:, n % W_SLOTS, c * P:(c + 1) * P], ident[:])
                ins.then_inc(turned, 1)

            def av_pe(pe, it, n, first, part):
                quad, i, _ = GROUPS[n % NG]
                if part == 0:
                    pe.wait_ge(wT_d, nth(NG, it, n))
                if n % GPQ == ROUND_ENDS[0] and part == 0:
                    pe.wait_ge(vq_d, nth(QUADS, it, n // GPQ))
                    if not (first and n < GPQ):
                        pe.wait_ge(oT_d, nth(QUADS, it, n // GPQ - 1))
                for j in range(part * AV_PART, min(i + 1, (part + 1) * AV_PART)):
                    for a in range(4):
                        ins = pe.matmul(bank[6][32 * a:32 * (a + 1), i * P:(i + 1) * P], vq[:, quad % 2, j, :],
                                        wT[:, round_of(n) % 2, a, j * P:(j + 1) * P],
                                        start=j == 0, stop=j == i, skip_group_check=True)
                if j == i:
                    ins.then_inc(av_d, 1)

            def back_pe(pe, it, quad):
                pe.wait_ge(oT_d, nth(QUADS, it, quad))
                for i in range(BPB):
                    ins = pe.transpose(bank[7][:, i * P:(i + 1) * P], oT[:, i * P:(i + 1) * P], ident[:])
                ins.then_inc(back, 1)

            def max_dve(v, it, n, h):
                _, i, heads = GROUPS[n]
                m = len(bank_items(n, h))
                v.wait_ge(scored, nth(2 * NG, it, half(n, h)))
                v.tensor_reduce(negm[:, n % 2, h, 0:m],
                                bank[2 * (n % 2) + h][:, 0:m * (i + 1) * P].rearrange("p (m c) -> p m c", m=m),
                                AX.X, ALU.max, negate=True).then_inc(maxed, 1)

            def exp_act(a_, it, n, h, first):
                quad, i, heads = GROUPS[n]
                a_.wait_ge(maxed, nth(2 * NG, it, half(n, h)))
                if h == 0:
                    if not (first and n < EX_SLOTS):
                        wait_w(a_, it, n - EX_SLOTS)
                    if n % GPQ == 0 and not (first and n < 2 * GPQ):
                        a_.wait_ge(den_d, nth(QUADS, it, n // GPQ - 2))
                for m, (k, st) in enumerate(bank_items(n, h)):
                    ins = a_.activation(ex_ap(n, i, k, st), s_ap(n, i, k, st), ACT.Exp,
                                        bias=negm[:, n % 2, h, m:m + 1],
                                        accum_out=Z[:, quad % 2, i * 4 + heads[k], st:st + 1])
                ins.then_inc(exped, 1)

            def of_heads(t, n, *more):
                quad, i, heads = GROUPS[n % NG]
                return t[(slice(None), quad % 2, slice(i * 4 + heads[0], i * 4 + heads[0] + len(heads))) + more]

            def recip_dve(v, it, n):
                v.wait_ge(exped, nth(2 * NG, it, half(n, 1)))
                v.reciprocal(rz2[:, n % 2, 0:len(GROUPS[n % NG][2])], of_heads(Z, n, 1)).then_inc(rz_d, 1)

            def coef_dve(v, it, n, first):
                if not (first and n < W_SLOTS):
                    v.wait_ge(turned, nth(NG, it, n - W_SLOTS))
                quad, i, heads = GROUPS[n % NG]
                h, s = len(heads), n % 2
                lam_h = nlam[:, quad * 4 + heads[0]:quad * 4 + heads[0] + h]
                v.wait_ge(rz_d, nth(NG, it, n))
                if h == 1:
                    v.scalar_tensor_tensor(out=coef[:, n % W_SLOTS, 0:1], in0=of_heads(Z, n, 0), scalar=rz2[:, s, 0:1], in1=lam_h,
                                           op0=ALU.mult, op1=ALU.mult).then_inc(coef_d, 1)
                else:
                    v.tensor_tensor(ratio[:, s, 0:h], of_heads(Z, n, 0), rz2[:, s, 0:h], ALU.mult).then_inc(ratio_d, 1)
                    v.wait_ge(ratio_d, nth(3 * QUADS, it, n // GPQ * 3 + (n % GPQ - 8)))
                    v.tensor_tensor(coef[:, n % W_SLOTS, 0:h], ratio[:, s, 0:h], lam_h, ALU.mult).then_inc(coef_d, 1)

            def sum_index(n):
                same = [g for g in range(GPQ) if abs_on_act(g) == abs_on_act(n)]
                return n // GPQ * len(same) + same.index(n % GPQ)

            def wait_w_slot(eng, it, n, first):
                if not (first and n < W_SLOTS):
                    eng.wait_ge(turned, nth(NG, it, n - W_SLOTS))
                    if abs_on_act(n - W_SLOTS):
                        eng.wait_ge(asum_a, nth(ACT_SUMS * QUADS, it, sum_index(n - W_SLOTS)))
                    elif on_pool(n):
                        eng.wait_ge(asum_d, nth(DVE_SUMS * QUADS, it, sum_index(n - W_SLOTS)))

            def w_dve(v, it, n, first):
                quad, i, heads = GROUPS[n % NG]
                v.wait_ge(coef_d, nth(NG, it, n))
                wait_w_slot(v, it, n, first)
                width = (i + 1) * P
                for k in range(len(heads)):
                    ins = v.scalar_tensor_tensor(out=w[:, n % W_SLOTS, k * width:(k + 1) * width], in0=ex_ap(n, i, k, 1),
                                                 scalar=coef[:, n % W_SLOTS, k:k + 1], in1=ex_ap(n, i, k, 0), op0=ALU.mult, op1=ALU.add)
                ins.then_inc(w_v, 1)

            def w_pool(pool, it, n, first):
                width = (GROUPS[n % NG][1] + 1) * P
                pool.wait_ge(coef_d, nth(NG, it, n))
                if not (first and w_index(n) == 0):
                    pool.wait_ge(w_p, nth(len(POOL_GROUPS) * QUADS, it, w_index(n) - 1))
                alone(pool)
                pool.tensor_scalar(e2c[:, 0:width], ex_ap(n, GROUPS[n % NG][1], 0, 1),
                                   coef[:, n % W_SLOTS, 0:1], 1.0, ALU.mult, ALU.mult).then_inc(e2c_d, 1)
                pool.wait_ge(e2c_d, nth(len(POOL_GROUPS) * QUADS, it, w_index(n)))
                wait_w_slot(pool, it, n, first)
                pool.tensor_tensor(w[:, n % W_SLOTS, 0:width], e2c[:, 0:width], ex_ap(n, GROUPS[n % NG][1], 0, 0), ALU.add).then_inc(w_p, 1)

            def abs_dve(v, it, n):
                _, i, heads = GROUPS[n % NG]
                wait_w(v, it, n)
                v.tensor_reduce(of_heads(asum, n), w[:, n % W_SLOTS, 0:len(heads) * (i + 1) * P].rearrange("p (h c) -> p h c", h=len(heads)),
                                AX.X, ALU.add, apply_absolute_value=True).then_inc(asum_d, 1)

            def abs_act(a_, it, n, first):
                _, i, heads = GROUPS[n % NG]
                cols = (i + 1) * P
                wait_w(a_, it, n)
                if not (first and sum_index(n) == 0):
                    a_.wait_ge(asum_a, nth(ACT_SUMS * QUADS, it, sum_index(n) - 1))
                a_.activation(absw[:, 0:cols], w[:, n % W_SLOTS, 0:cols], ACT.Abs, accum_out=of_heads(asum, n)).then_inc(asum_a, 1)

            def copy_wT_act(a_, it, n, first):
                _, i, heads = GROUPS[n % NG]
                h, cols = len(heads), (i + 1) * P
                a_.wait_ge(turned, nth(NG, it, n))
                if starts_round(n) and not (first and round_of(n) < 2):
                    a_.wait_ge(av_d, nth(ROUNDS, it, round_of(n) - 2))
                a_.copy(wT[:, round_of(n) % 2, heads[0]:heads[0] + h, 0:cols],
                        bank[4 + n % 2][:, 0:h * cols].rearrange("p (h c) -> p h c", h=h)).then_inc(wT_d, 1)

            def copy_oT_act(a_, it, quad, first):
                a_.wait_ge(av_d, nth(ROUNDS, it, (quad + 1) * len(ROUND_ENDS) - 1))
                if not (first and quad == 0):
                    a_.wait_ge(back, nth(QUADS, it, quad - 1))
                a_.copy(oT[:], bank[6][:]).then_inc(oT_d, 1)

            def finish_quad_dve(v, it, quad, first):
                q = quad % 2
                v.wait_ge(asum_d, nth(DVE_SUMS * QUADS, it, (quad + 1) * DVE_SUMS - 1))
                v.wait_ge(asum_a, nth(ACT_SUMS * QUADS, it, (quad + 1) * ACT_SUMS - 1))
                v.scalar_tensor_tensor(out=den[:, q, :], in0=Z[:, q, :, 0], scalar=DENOM_MIN, in1=asum[:, q, :],
                                       op0=ALU.mult, op1=ALU.max).then_inc(den_d, 1)
                v.wait_ge(den_d, nth(QUADS, it, quad))
                v.reciprocal(rden[:, q, :], den[:, q, :]).then_inc(rden_d, 1)
                v.wait_ge(rden_d, nth(QUADS, it, quad))
                v.wait_ge(back, nth(QUADS, it, quad))
                if quad == 0 and not first:
                    v.wait_ge(obT_p, it)
                qq = quad % QUADS
                for a in range(4):
                    ins = v.tensor_tensor(ob[:, :, (qq * 4 + a) * HD:(qq * 4 + a + 1) * HD],
                                          bank[7][:].rearrange("p (i c) -> p i c", c=P)[:, :, 40 * a:40 * a + HD],
                                          rden[:, q, :].rearrange("p (i a o) -> p i a o", i=4, o=1)[:, :, a].to_broadcast([P, BPB, HD]),
                                          ALU.mult)
                ins.then_inc(ob_d, 1)

            BACK = FINISH_STEP - 1
            NEXT_NORM, NEXT_Q, NEXT_K1, NEXT_K2, NEXT_V = 3, 16, 21, 24, 35
            OUT_TURN, OUT_PROJ, ROUTE_NORM, ROUTE_SCORE, ROUTE_RANK = 10, 13, 27, 32, 38
            TAIL = ROUTE_RANK + 6

            def steps(eng, body):
                body(eng, 0, True, False, False)
                with eng.Fori(1, BATCH - 1) as it:
                    body(eng, it, False, False, False)
                body(eng, BATCH - 1, False, True, False)
                body(eng, BATCH, False, False, True)

            def runs(n, first, tail):
                return (n >= 0 and not tail) or (n < 0 and not first)

            def quad_done(n, after, first, tail):
                return n % GPQ == after and runs(n - after - 1, first, tail)

            def body_pe(pe, it, first, last, tail):
                nxt = not (last or tail)
                for n in range(TAIL if tail else NG):
                    if runs(n, first, tail):
                        scores_pe(pe, it, n, first)
                    if runs(n - TURN_LAG, first, tail):
                        turn_pe(pe, it, n - TURN_LAG, first)
                    for part in range(2):
                        end = n - AV_LAG - part
                        if end % GPQ in ROUND_ENDS and runs(end, first, tail) and part * AV_PART <= GROUPS[end % NG][1]:
                            av_pe(pe, it, end, first, part)
                    if n == NEXT_NORM and nxt:
                        if not first:
                            pe.wait_ge(ob_d, nth(QUADS, it, -2))
                        norm.pe(pe, it + 1, 0)
                    if quad_done(n, BACK, first, tail):
                        quad = n // GPQ - 1
                        if quad == -1:
                            if nxt:
                                pe.wait_ge(norm.xnT, it + 2)
                            else:
                                pe.wait_ge(ob_d, nth(QUADS, it, -2))
                        if quad == 0:
                            if nxt:
                                pe.wait_ge(res1, 3 * it + (3 + 1))
                            else:
                                pe.wait_ge(x_d, it)
                        if quad == 1:
                            if first:
                                pe.wait_ge(res1, 3 * it + (3 + 3))
                            else:
                                pe.wait_ge(routing.norm.xnT, it)
                        if quad == 2:
                            if first:
                                pe.wait_ge(v_d, it + 2)
                            else:
                                pe.wait_ge(routing.place, it)
                        back_pe(pe, it, quad)
                    if n == OUT_TURN and not first:
                        pe.wait_ge(ob_d, nth(QUADS, it, -1))
                        for j in range(BPB):
                            ins = pe.transpose(bank[7][:, j * P:(j + 1) * P], ob[:, j, :], ident[:])
                        ins.then_inc(obT_p, 1)
                    if n == OUT_PROJ and not first:
                        pe.wait_ge(obT_d, it)
                        for j in range(BPB):
                            ins = pe.matmul(bank[7][:, j * P:(j + 1) * P], obT[:, j * P:(j + 1) * P], WT[:, 4, :], start=True, stop=True)
                        ins.then_inc(op_p, 1)
                    if n == NEXT_Q and nxt:
                        if not first:
                            pe.wait_ge(x_d, it)
                        proj_pe(pe, it + 1, 0)
                    if n == NEXT_K1 and nxt:
                        pe.wait_ge(ob_d, nth(QUADS, it, 0))
                        proj_pe(pe, it + 1, 1)
                    if n == NEXT_K2 and nxt:
                        pe.wait_ge(res1, 3 * it + (3 + 2))
                        proj_pe(pe, it + 1, 2)
                    if n == ROUTE_NORM and not first:
                        if nxt:
                            pe.wait_ge(res1, 3 * it + (3 + 3))
                        if last:
                            pe.wait_ge(ob_d, nth(QUADS, it, 0))
                        if tail:
                            pe.wait_ge(x_d, it)
                        routing.norm.pe(pe, it - 1, 1)
                    if n == ROUTE_SCORE and not first:
                        if not tail:
                            pe.wait_ge(ob_d, nth(QUADS, it, 1))
                        routing.score_pe(pe, it - 1, 1)
                    if n == NEXT_V and nxt:
                        if first:
                            pe.wait_ge(ob_d, nth(QUADS, it, 1))
                        else:
                            pe.wait_ge(routing.rsc, it)
                        v_pe(pe, it + 1)
                    if n == ROUTE_RANK and not first:
                        if nxt:
                            pe.wait_ge(v_d, it + 2)
                        else:
                            pe.wait_ge(routing.rsc, it)
                        routing.rank_pe(pe, it - 1, 1)

            def body_act(a, it, first, last, tail):
                nxt = not (last or tail)
                for n in range(TAIL if tail else NG):
                    if runs(n, first, tail):
                        exp_act(a, it, n, 0, first)
                    if runs(n - TURN_LAG, first, tail):
                        copy_wT_act(a, it, n - TURN_LAG, first)
                    if runs(n, first, tail):
                        exp_act(a, it, n, 1, first)
                    if abs_on_act(n - ABS_LAG) and runs(n - ABS_LAG, first, tail):
                        abs_act(a, it, n - ABS_LAG, first)
                    if quad_done(n, FINISH_STEP - 2, first, tail):
                        copy_oT_act(a, it, n // GPQ - 1, first)
                    if n == NEXT_NORM + 1 and nxt:
                        norm.act(a, it + 1, 0)
                    if n == OUT_TURN + 1 and not first:
                        a.wait_ge(obT_p, it)
                        a.copy(obT[:], bank[7][:]).then_inc(obT_d, 1)
                    for t, at in enumerate((NEXT_Q, NEXT_K1, NEXT_K2)):
                        if n == at + 1 and nxt:
                            high_act(a, it + 1, t)
                        if n == at + 2 and nxt:
                            middle_act(a, it + 1, t)
                    if n == NEXT_V + 1 and nxt:
                        v_act(a, it + 1)
                    if n == ROUTE_NORM + 1 and not first:
                        routing.norm.act(a, it - 1, 1)

            def body_dve(v, it, first, last, tail):
                nxt = not (last or tail)
                for n in range(TAIL if tail else NG):
                    if runs(n, first, tail):
                        max_dve(v, it, n, 0)
                    if runs(n - W_LAG, first, tail):
                        recip_dve(v, it, n - W_LAG)
                    if runs(n, first, tail):
                        max_dve(v, it, n, 1)
                    if n == ROUTE_SCORE + 2 and not first:
                        routing.max_dve(v, it - 1, 1)
                    if n == ROUTE_SCORE + 3 and not first:
                        routing.cand_dve(v, it - 1, 1)
                    if n == ROUTE_SCORE + 4 and not first:
                        routing.onehot_dve(v, it - 1, 1)
                    if runs(n - W_LAG, first, tail):
                        coef_dve(v, it, n - W_LAG, first)
                    if not abs_on_act(n - ABS_LAG) and runs(n - ABS_LAG, first, tail):
                        abs_dve(v, it, n - ABS_LAG)
                    if runs(n - W_LAG, first, tail) and not on_pool(n - W_LAG):
                        w_dve(v, it, n - W_LAG, first)
                    if quad_done(n, FINISH_STEP, first, tail):
                        finish_quad_dve(v, it, n // GPQ - 1, first)
                    if n == NEXT_NORM - 3 and nxt:
                        norm.dve_stats(v, it + 1, 0)
                    if n == NEXT_NORM - 1 and nxt:
                        norm.dve_apply(v, it + 1, 0)
                    if n == OUT_PROJ + 1 and not first:
                        v.wait_ge(op_p, it)
                        xb = X[:, bass.ds((it - 1) * BPB, BPB), :]
                        v.tensor_tensor(xb, bank[7][:].rearrange("p (j d) -> p j d", d=D), xb, ALU.add).then_inc(x_d, 1)
                    for t, at in enumerate((NEXT_Q, NEXT_K1, NEXT_K2)):
                        if n == at + 1 and nxt:
                            rest_dve(v, it + 1, t)
                        if n == at + 5 and nxt:
                            low_dve(v, it + 1, t)
                    if n == OUT_PROJ + 2 and not first:
                        v.wait_ge(x_d, it)
                        alone(v)
                        routing.norm.dve_stats(v, it - 1, 1)
                    if n == ROUTE_NORM - 2 and not first:
                        routing.norm.dve_apply(v, it - 1, 1)
                    if n == ROUTE_SCORE + 1 and not first:
                        routing.score_dve(v, it - 1, 1)
                    if n == ROUTE_SCORE + 2 and not first:
                        routing.equal_dve(v, it - 1, 1)
                    if n == ROUTE_SCORE + 3 and not first:
                        routing.min_dve(v, it - 1, 1)
                    if n == ROUTE_SCORE + 4 and not first:
                        routing.sum_dve(v, it - 1, 1)
                    if n == ROUTE_RANK + 1 and not first:
                        routing.place_dve(v, it - 1, 1)
                    if n == ROUTE_RANK + 2 and not first:
                        routing.seen_dve(v, it - 1, 1)
                    if n == ROUTE_RANK + 3 and not first:
                        routing.picked_dve(v, it - 1, 1)
                    if n == ROUTE_RANK + 4 and not first:
                        routing.slot_dve(v, it - 1, 1)
                    if n == ROUTE_RANK + 5 and not first:
                        routing.slotu_dve(v, it - 1, 1)

            def load_sp(sp, it, quad, first):
                s = quad % 2
                if not (first and quad < 2):
                    sp.wait_ge(scored, nth(2 * NG, it, half((quad - 1) * GPQ - 1, 1)))
                for t in range(3):
                    for par in range(2):
                        sp.dma_start(stack[64 * par:64 * par + ROWS, s, t, :, :],
                                     KD[t, bass.ds(it, 1), :, (quad * 2 + par) * 2 * HD:(quad * 2 + par + 1) * 2 * HD, :].rearrange(
                                         "b m (d h) n -> (b m) d (h n)", h=2)
                                     ).then_inc(loaded[s], 16)

            def body_sp(sp, it, first, last, tail):
                if tail:
                    return
                sp.wait_ge(kd_out, (it + 1) * (3 * 3 * 16))
                load_sp(sp, it, 0, first)
                load_sp(sp, it, 1, first)
                load_sp(sp, it, 2, first)
                if not last:
                    store_sp(sp, it + 1, 0)
                    store_sp(sp, it + 1, 1)
                load_sp(sp, it, 3, first)
                if not last:
                    store_sp(sp, it + 1, 2)

            def vq_pool(pool, b, quad, wait):
                pool.wait_ge(v_d, b + 1)
                if wait:
                    pool.wait_ge(av_d, nth(ROUNDS, b, (quad - 1) * len(ROUND_ENDS) - 1))
                alone(pool)
                pool.tensor_copy(vq[:, quad % 2], V[:, bass.ds(b * BPB, BPB), quad * 32:(quad + 1) * 32]).then_inc(vq_d, 1)

            def body_pool(pool, it, first, last, tail):
                nxt = not (last or tail)
                for n in range(TAIL if tail else NG):
                    if n == 1 and nxt:
                        norm.pool(pool, it + 1, 0)
                    if runs(n - W_LAG, first, tail) and on_pool(n - W_LAG):
                        w_pool(pool, it, n - W_LAG, first)
                    if n % GPQ == GPQ - 3 and not tail:
                        quad = n // GPQ + 1
                        if quad < QUADS:
                            vq_pool(pool, it, quad, not (first and quad < 2))
                        elif nxt:
                            vq_pool(pool, it + 1, 0, True)
                    if n == OUT_PROJ + 3 and not first:
                        routing.norm.pool(pool, it - 1, 1)
                    if n == ROUTE_RANK + 5 and not first:
                        routing.scatter_pool(pool, it - 1, 1)
                        pool.wait_ge(routing.scattered[1], it * (16 * BPB))

            def sp_part(sp):
                for t in range(3):
                    store_sp(sp, 0, t)
                steps(sp, body_sp)

            def pool_part(pool):
                norm.pool(pool, 0, 0)
                vq_pool(pool, 0, 0, False)
                steps(pool, body_pool)

            def dve_part(v):
                routing.start_dve(v)
                v.wait_ge(x_ready, BATCH)
                norm.dve_stats(v, 0, 0)
                norm.dve_apply(v, 0, 0)
                for t in range(4):
                    if t < 3:
                        rest_dve(v, 0, t, bank[t])
                    if t > 0:
                        low_dve(v, 0, t - 1)
                steps(v, body_dve)

            def act_part(a):
                norm.act(a, 0, 0)
                for t in range(4):
                    if t < 3:
                        high_act(a, 0, t, bank[t])
                    if t > 0:
                        middle_act(a, 0, t - 1)
                v_act(a, 0, bank[3])
                steps(a, body_act)

            def pe_part(pe):
                norm.pe(pe, 0, 0)
                for t in range(3):
                    proj_pe(pe, 0, t, bank[t])
                v_pe(pe, 0, bank[3])
                pe.wait_ge(res1, 3)
                pe.wait_ge(v_d, 1)
                steps(pe, body_pe)

            return dict(sp=sp_part, pool=pool_part, dve=dve_part, act=act_part, pe=pe_part)

        route1 = Routing("f1", bank[0:2] * 2, bank[2:4] * 2, bank[4:6] * 2)

        def route_dve(v):
            route1.start_dve(v)
            for b in range(BATCH + 2):
                if b < BATCH:
                    v.wait_ge(x_in[b], 16)
                    route1.norm.dve_stats(v, b, b)
                if b == 0:
                    setup_biases_dve(v)
                    v.wait_ge(pool_set, NSET_POOL)
                if 1 <= b <= BATCH:
                    route1.norm.dve_apply(v, b - 1, b - 1)
                if b >= 2:
                    for stage in (route1.score_dve, route1.max_dve, route1.equal_dve, route1.cand_dve, route1.min_dve,
                                  route1.onehot_dve, route1.sum_dve, route1.place_dve, route1.seen_dve,
                                  route1.picked_dve, route1.slot_dve, route1.slotu_dve):
                        stage(v, b - 2, b - 2)

        def route_pe(pe):
            for b in range(BATCH + 1):
                if b < BATCH:
                    route1.norm.pe(pe, b, b)
                    route1.score_pe(pe, b, b)
                if b >= 1:
                    route1.rank_pe(pe, b - 1, b - 1)

        def route_act(a):
            for b in range(BATCH):
                route1.norm.act(a, b, b)

        def route_pool(pool):
            for b in range(BATCH + 2):
                if b < BATCH:
                    route1.norm.pool(pool, b, b)
                if b >= 2:
                    route1.scatter_pool(pool, b - 2, b - 2)

        route2 = Routing("f2", [bank[7]] * 2, [bank[7]] * 2, [bank[7]] * 2)

        ffn1, x1 = ffn("f1", route1, (BPB,) * BATCH, False)
        attn = attention(x1, route2)
        ffn2, _ = ffn("f2", route2, (0, NBLK) + (0,) * (BATCH - 2), True)

        block = ctx.enter_context(nc.Block())

        @block.sync
        def _(sp):
            setup_sp(sp)
            ffn1["sp"](sp)
            attn["sp"](sp)
            ffn2["sp"](sp)

        @block.gpsimd
        def _(pool):
            setup_pool(pool)
            route_pool(pool)
            ffn1["pool"](pool)
            attn["pool"](pool)
            ffn2["pool"](pool)

        @block.vector
        def _(v):
            route_dve(v)
            setup_dve(v)
            ffn1["dve"](v)
            attn["dve"](v)
            ffn2["dve"](v)

        @block.scalar
        def _(a):
            route_act(a)
            setup_act(a)
            ffn1["act"](a)
            attn["act"](a)
            ffn2["act"](a)

        @block.tensor
        def _(pe):
            pe.wait_ge(pool_set, NSET_POOL)
            pe.wait_ge(small_in, 16 * 10)
            route_pe(pe)
            setup_pe(pe)
            pe.wait_ge(dve_set, DVE_SET)
            ffn1["pe"](pe)
            attn["pe"](pe)
            ffn2["pe"](pe)


_INS = ["L0_attn_x", "L0_attn_Wq", "L0_attn_Wk1", "L0_attn_Wk2", "L0_attn_Wv", "L0_attn_Wo", "L0_attn_lambda_logit",
        "L0_ffn_wr", "L0_ffn_br", "L0_ffn_w1", "L0_ffn_b1", "L0_ffn_w2", "L0_ffn_b2"]


def kernel(**inputs):
    import numpy as _np
    import concourse.bacc as _bacc
    from concourse import mybir as _mybir
    from concourse.bass_utils import run_bass_kernel_spmd as _run

    nc = _bacc.Bacc("TRN2", target_bir_lowering=False, num_devices=1)
    arrays, args = {}, []
    for name in _INS:
        a = _np.ascontiguousarray(inputs[name])
        arrays[f"in_{name}_dram"] = a
        args.append(nc.dram_tensor(f"in_{name}_dram", a.shape, _mybir.dt.from_np(a.dtype), kind="ExternalInput").ap())
    out = nc.dram_tensor("out_0_dram", (BATCH, SEQ, D), _mybir.dt.float32, kind="ExternalOutput").ap()
    build(nc, *args, out)
    r = _run(nc, [arrays], core_ids=[0])
    return r.results[0]["out_0_dram"]
```
